# Optimizing a Trainium2 kernel written in Bass

```python
import numpy as np
import jax
import jax.numpy as jnp

def _softmax(x, axis=-1):
    return jax.nn.softmax(x, axis=axis)

def _gelu(x):
    return jax.nn.gelu(x, approximate=True)

def _silu(x):
    return jax.nn.silu(x)

def _sigmoid(x):
    return jax.nn.sigmoid(x)

def _layernorm(x, axis=-1, eps=1e-05):
    m = jnp.mean(x, axis=axis, keepdims=True)
    v = jnp.var(x, axis=axis, keepdims=True)
    return (x - m) / jnp.sqrt(v + eps)

def _scatter_add(tgt, idx, src, axis=0):
    return tgt.at[idx].add(src)

def _segment_sum(src, seg, n):
    return jax.ops.segment_sum(src, seg, n)
kernel_name = 'mk_gnn_preln_d4_gnn_r32_df30d0'

def setup_inputs(seed: int=0):
    np.random.seed(seed)
    _w = jnp.asarray

    def _rec_inputs():
        import jax
        import jax.numpy as jnp
        _gk = jax.random.key(seed)
        x = -0.000202 + 1 * jax.random.normal(jax.random.fold_in(_gk, 1), (3125, 64), jnp.float32)
        _s = jax.random.randint(jax.random.fold_in(_gk, 2), (50000,), 0, 3125, jnp.int32)
        _d = jax.random.randint(jax.random.fold_in(_gk, 3), (50000,), 0, 3125, jnp.int32)
        _loop = jnp.arange(3125, dtype=jnp.int32)
        src = jnp.concatenate([_s, _d, _loop])
        dst = jnp.concatenate([_d, _s, _loop])
        _o = jnp.argsort(dst, stable=True)
        src = src[_o]
        dst = dst[_o]
        edge_type_16 = jax.random.randint(jax.random.fold_in(_gk, 13), (103125,), 0, 16, jnp.int32)
        edge_weight = jax.random.uniform(jax.random.fold_in(_gk, 14), (103125,), jnp.float32, 0.0, 1)
        return (x, src, dst, edge_type_16, edge_weight)
    x, src, dst, edge_type_16, edge_weight = _rec_inputs()

    def _L0_gnn_setup():
        import jax, jax.numpy as jnp
        import numpy as np
        N_NODES = 3125
        key = jax.random.key(seed)
        ks = jax.random.split(key, 11)
        d_in, d_out = (64, 64)
        n_edges = 50000
        x = jax.random.normal(ks[0], (N_NODES, d_in), dtype=jnp.float32)
        edge_index = jax.random.randint(ks[1], (2, n_edges), 0, N_NODES, dtype=jnp.int64)
        s = 1.0 / np.sqrt(d_in)
        return {'x': x, 'edge_index': edge_index, 'W_key': jax.random.normal(ks[2], (d_in, d_out), dtype=jnp.float32) * s, 'b_key': jax.random.normal(ks[3], (d_out,), dtype=jnp.float32) * s, 'W_query': jax.random.normal(ks[4], (d_in, d_out), dtype=jnp.float32) * s, 'b_query': jax.random.normal(ks[5], (d_out,), dtype=jnp.float32) * s, 'W_value': jax.random.normal(ks[6], (d_in, d_out), dtype=jnp.float32) * s, 'b_value': jax.random.normal(ks[7], (d_out,), dtype=jnp.float32) * s, 'W_skip': jax.random.normal(ks[8], (d_in, d_out), dtype=jnp.float32) * s, 'b_skip': jax.random.normal(ks[9], (d_out,), dtype=jnp.float32) * s}
    _L0_gnn_all = _L0_gnn_setup()
    _L0_gnn_in = {k: v for k, v in _L0_gnn_all.items() if k in ('W_key', 'b_key', 'W_query', 'b_query', 'W_value', 'b_value', 'W_skip', 'b_skip')}
    del _L0_gnn_all

    def _L1_gnn_setup():
        import jax, jax.numpy as jnp
        import numpy as np
        N_NODES = 3125
        N_EDGES = 50000
        IN_DIM = 64
        HID = 64

        def sage_conv(x, src, dst, W_l, b_l, W_r):
            n = x.shape[0]
            msg_sum = jax.ops.segment_sum(x[src], dst, num_segments=n)
            cnt = jax.ops.segment_sum(jnp.ones((src.shape[0],), x.dtype), dst, num_segments=n)
            mean = msg_sum / jnp.maximum(cnt, 1.0)[:, None]
            return mean @ W_l + b_l + x @ W_r
        key = jax.random.key(seed)
        k = jax.random.split(key, 8)
        x = jax.random.normal(k[0], (N_NODES, IN_DIM), dtype=jnp.float32)
        edge_index = jax.random.randint(k[1], (2, N_EDGES), 0, N_NODES, dtype=jnp.int64 if jax.config.read('jax_enable_x64') else jnp.int32)
        s1 = 1.0 / np.sqrt(IN_DIM)
        s2 = 1.0 / np.sqrt(2 * HID)
        W1_l = jax.random.uniform(k[2], (IN_DIM, 2 * HID), jnp.float32, -s1, s1)
        W1_r = jax.random.uniform(k[3], (IN_DIM, 2 * HID), jnp.float32, -s1, s1)
        b1 = jax.random.uniform(k[4], (2 * HID,), jnp.float32, -s1, s1)
        W2_l = jax.random.uniform(k[5], (2 * HID, HID), jnp.float32, -s2, s2)
        W2_r = jax.random.uniform(k[6], (2 * HID, HID), jnp.float32, -s2, s2)
        b2 = jax.random.uniform(k[7], (HID,), jnp.float32, -s2, s2)
        return {'x': x, 'edge_index': edge_index, 'W1_l': W1_l, 'b1': b1, 'W1_r': W1_r, 'W2_l': W2_l, 'b2': b2, 'W2_r': W2_r}
    _L1_gnn_all = _L1_gnn_setup()
    _L1_gnn_in = {k: v for k, v in _L1_gnn_all.items() if k in ('W1_l', 'b1', 'W1_r', 'W2_l', 'b2', 'W2_r')}
    del _L1_gnn_all

    def _L2_gnn_setup():
        import jax, jax.numpy as jnp
        import numpy as np
        N_NODES = 3125
        N_EDGES = 31250
        D_IN = 64
        D_OUT = 64
        N_RELS = 16
        key = jax.random.key(seed)
        k1, k2, k3, k4, k5 = jax.random.split(key, 5)
        feat = jax.random.normal(k1, (N_NODES, D_IN), dtype=jnp.float32)
        weight = jax.random.normal(k2, (N_RELS, D_IN, D_OUT), dtype=jnp.float32) * 0.05
        src = jax.random.randint(k3, (N_EDGES,), 0, N_NODES)
        dst = jax.random.randint(k4, (N_EDGES,), 0, N_NODES)
        etypes = jax.random.randint(k5, (N_EDGES,), 0, N_RELS)
        return {'feat': feat, 'weight': weight, 'src': src, 'dst': dst, 'etypes': etypes}
    _L2_gnn_all = _L2_gnn_setup()
    _L2_gnn_in = {k: v for k, v in _L2_gnn_all.items() if k in ('weight',)}
    del _L2_gnn_all

    def _L3_gnn_setup():
        import jax, jax.numpy as jnp
        import numpy as np
        N = 8192
        E = 65536
        D = 64
        K = 3
        key = jax.random.key(seed)
        k1, k2, k3, k4 = jax.random.split(key, 4)
        embeddings = jax.random.normal(k1, (N, D), dtype=jnp.float32)
        rows = jnp.sort(jax.random.randint(k2, (E,), 0, N, dtype=jnp.int64))
        cols = jax.random.randint(k3, (E,), 0, N, dtype=jnp.int64)
        vals = jax.random.uniform(k4, (E,), dtype=jnp.float32)
        return {'embeddings': embeddings, 'vals': vals, 'rows': rows, 'cols': cols, 'k': K}
    _L3_gnn_all = _L3_gnn_setup()
    _L3_gnn_in = {k: v for k, v in _L3_gnn_all.items() if k in ()}
    del _L3_gnn_all
    return {'x': x, 'src': src, 'dst': dst, 'edge_type_16': edge_type_16, 'edge_weight': edge_weight, 'L0_gnn_W_key': _L0_gnn_in['W_key'], 'L0_gnn_b_key': _L0_gnn_in['b_key'], 'L0_gnn_W_query': _L0_gnn_in['W_query'], 'L0_gnn_b_query': _L0_gnn_in['b_query'], 'L0_gnn_W_value': _L0_gnn_in['W_value'], 'L0_gnn_b_value': _L0_gnn_in['b_value'], 'L0_gnn_W_skip': _L0_gnn_in['W_skip'], 'L0_gnn_b_skip': _L0_gnn_in['b_skip'], 'L1_gnn_W1_l': _L1_gnn_in['W1_l'], 'L1_gnn_b1': _L1_gnn_in['b1'], 'L1_gnn_W1_r': _L1_gnn_in['W1_r'], 'L1_gnn_W2_l': _L1_gnn_in['W2_l'], 'L1_gnn_b2': _L1_gnn_in['b2'], 'L1_gnn_W2_r': _L1_gnn_in['W2_r'], 'L2_gnn_weight': _L2_gnn_in['weight']}

def reference(x, src, dst, edge_type_16, edge_weight, L0_gnn_W_key, L0_gnn_b_key, L0_gnn_W_query, L0_gnn_b_query, L0_gnn_W_value, L0_gnn_b_value, L0_gnn_W_skip, L0_gnn_b_skip, L1_gnn_W1_l, L1_gnn_b1, L1_gnn_W1_r, L1_gnn_W2_l, L1_gnn_b2, L1_gnn_W2_r, L2_gnn_weight):
    import jax
    import jax.numpy as jnp

    def _L0_gnn_ref(x, edge_index, W_key, b_key, W_query, b_query, W_value, b_value, W_skip, b_skip):
        import jax, jax.numpy as jnp
        import numpy as np
        N_NODES = 3125
        k = x @ W_key + b_key
        q = x @ W_query + b_query
        v = x @ W_value + b_value
        src = edge_index[0]
        dst = edge_index[1]
        gate = jax.nn.sigmoid(k[dst] + q[src])
        msg = gate * v[src]
        agg = jax.ops.segment_sum(msg, dst, num_segments=N_NODES)
        return agg + x @ W_skip + b_skip

    def _L1_gnn_ref(x, edge_index, W1_l, b1, W1_r, W2_l, b2, W2_r):
        import jax, jax.numpy as jnp
        import numpy as np
        N_NODES = 3125
        N_EDGES = 50000
        IN_DIM = 64
        HID = 64

        def sage_conv(x, src, dst, W_l, b_l, W_r):
            n = x.shape[0]
            msg_sum = jax.ops.segment_sum(x[src], dst, num_segments=n)
            cnt = jax.ops.segment_sum(jnp.ones((src.shape[0],), x.dtype), dst, num_segments=n)
            mean = msg_sum / jnp.maximum(cnt, 1.0)[:, None]
            return mean @ W_l + b_l + x @ W_r
        src, dst = (edge_index[0], edge_index[1])
        h = jax.nn.relu(sage_conv(x, src, dst, W1_l, b1, W1_r))
        h = jax.nn.relu(sage_conv(h, src, dst, W2_l, b2, W2_r))
        return h

    def _L2_gnn_ref(feat, weight, src, dst, etypes):
        import jax, jax.numpy as jnp
        import numpy as np
        N_NODES = 3125
        N_EDGES = 31250
        D_IN = 64
        D_OUT = 64
        N_RELS = 16
        h = feat[src]
        n_rels = weight.shape[0]
        e, d_out = (h.shape[0], weight.shape[2])

        def step(m, rw):
            r, w_r = rw
            mask = jnp.where(etypes == r, 1.0, 0.0).astype(h.dtype)
            m = m + mask[:, None] * (h @ w_r)
            return (m, None)
        m0 = jnp.zeros((e, d_out), dtype=h.dtype)
        m, _ = jax.lax.scan(step, m0, (jnp.arange(n_rels), weight))
        out = jax.ops.segment_sum(m, dst, num_segments=feat.shape[0])
        return out

    def _L3_gnn_ref(embeddings, vals, rows, cols, k):
        import jax, jax.numpy as jnp
        import numpy as np
        N = 8192
        E = 65536
        D = 64
        K = 3
        'LightGCN propagation: mean over {x, Sx, S^2 x, ..., S^k x}.'
        n = embeddings.shape[0]

        def spmm(x):
            return jax.ops.segment_sum(vals[:, None] * x[cols], rows, num_segments=n)
        x = embeddings
        acc = x
        for _ in range(k):
            x = spmm(x)
            acc = acc + x
        return acc / (k + 1)
    edge_index = jnp.stack([src, dst])
    h = jnp.maximum(_layernorm(x, axis=-1), 0.0)
    x = x + _L0_gnn_ref(h, edge_index, L0_gnn_W_key, L0_gnn_b_key, L0_gnn_W_query, L0_gnn_b_query, L0_gnn_W_value, L0_gnn_b_value, L0_gnn_W_skip, L0_gnn_b_skip)
    h = jnp.maximum(_layernorm(x, axis=-1), 0.0)
    x = x + _L1_gnn_ref(h, edge_index, L1_gnn_W1_l, L1_gnn_b1, L1_gnn_W1_r, L1_gnn_W2_l, L1_gnn_b2, L1_gnn_W2_r)
    h = jnp.maximum(_layernorm(x, axis=-1), 0.0)
    x = x + _L2_gnn_ref(h, L2_gnn_weight, src, dst, edge_type_16)
    h = jnp.maximum(_layernorm(x, axis=-1), 0.0)
    x = x + _L3_gnn_ref(h, edge_weight, src, dst, 3)
    return x

_drawn_inputs = setup_inputs


def setup_inputs(seed=0):
    import zlib

    import numpy as np

    out = dict(_drawn_inputs(seed))
    spreads = {}
    factors = {'L0_gnn_b_skip': 3.895,
     'L1_gnn_W1_l': 3.545,
     'L1_gnn_b1': 8.0,
     'L1_gnn_W1_r': 4.343,
     'L1_gnn_W2_l': 3.369,
     'L1_gnn_b2': 8.0,
     'L1_gnn_W2_r': 3.728,
     'x': 2.698}
    for name, (base, spread) in spreads.items():
        noise = np.random.default_rng([zlib.crc32(name.encode()), seed]).standard_normal(out[name].shape)
        drawn = base * np.exp(spread * noise) if base else spread * noise
        out[name] = jnp.asarray(drawn.astype(out[name].dtype))
    for name, factor in factors.items():
        out[name] = (out[name] * factor).astype(out[name].dtype)
    return out
```

```python
from contextlib import ExitStack

import concourse.bass as bass
from concourse import mybir

N = 3125
D = 64
HID = 128
E = 103125
R = 16
P = 128
BLOCKS = -(-N // P)
FULL_BLOCKS = N // P
TAIL = N - FULL_BLOCKS * P
NPAD = BLOCKS * P
GROUP = 8
SLOTS = 3
TILES = -(-E // (P * GROUP * SLOTS)) * GROUP * SLOTS
ITERS = TILES // (GROUP * SLOTS)
CHUNKS = -(-TILES // P)
CHUNK_TILES = CHUNKS * P
WINDOW = 2 * P
WINDOWS = (BLOCKS + 1) // 2
BANK = 512
ACC_BANKS = 4
CNT0 = 2 * WINDOWS * D
PER_BANK = BANK // P
TCHUNKS = -(-BLOCKS // PER_BANK)
EPS = 1e-5
PASSES = 7
FAR = 4096.0


def build(nc, x, src, dst, etype, weight, w_key, b_key, w_query, b_query, w_value, b_value,
          w_skip, b_skip, w1_l, b1, w1_r, w2_l, b2, w2_r, w_rel, out):
    f32 = mybir.dt.float32
    i32 = mybir.dt.int32
    bf16 = mybir.dt.bfloat16
    ALU = mybir.AluOpType
    ACT = mybir.ActivationFunctionType
    AX = mybir.AxisListType

    ctx = ExitStack()
    with ctx:
        def sb(name, shape, dt=f32):
            return ctx.enter_context(nc.sbuf_tensor(name, shape, dt))

        def sem(name):
            return ctx.enter_context(nc.semaphore(name))

        def dram(name, shape, dt=f32):
            return nc.dram_tensor(name, shape, dt, kind="Internal").ap()

        key_tab = dram("key_tab", [NPAD, D])
        qv_tab = dram("qv_tab", [NPAD, 2 * D])
        rel_tab = dram("rel_tab", [NPAD * R, D])
        node_tab = [dram(f"node_tab{p}", [NPAD, D]) for p in range(PASSES)]
        block_d = dram("block_d", [CHUNKS, P], i32)

        EARLY = CHUNKS * P
        early = sb("early", [P, 11 * EARLY])

        def field_at(k):
            return early[:, k * EARLY:(k + 1) * EARLY].rearrange("p (j q) -> p j q", q=P)

        dst_raw = field_at(0).bitcast(i32)
        src_raw = field_at(1).bitcast(i32)
        et_raw = field_at(2).bitcast(i32)
        w_raw = field_at(3)
        dst_f = field_at(4)
        src_f = field_at(5)
        et_f = field_at(6)
        rel_f = field_at(7)
        key_f = field_at(8)
        loc_f = field_at(9)
        inside = field_at(10)
        mT = early[0:D, 0:NPAD]
        gT = early[:, NPAD:2 * NPAD]
        rows = early[:, 2 * NPAD:2 * NPAD + SLOTS * GROUP * D].rearrange("p (s j d) -> p s j d", s=SLOTS, d=D)
        key_rows = early[:, 2 * NPAD + SLOTS * GROUP * D:2 * NPAD + 2 * SLOTS * GROUP * D].rearrange("p (s j d) -> p s j d", s=SLOTS, d=D)
        tile_min = sb("tile_min", [P, CHUNKS])
        min_i = sb("min_i", [P, CHUNKS], i32)
        block_i = sb("block_i", [P, CHUNKS], i32)
        block_f = sb("block_f", [P, CHUNKS])
        base_f = sb("base_f", [P, CHUNKS])
        n_inside = sb("n_inside", [P, 1])
        spread = sb("spread", [1, 1], i32)
        block_t = sb("block_t", [CHUNKS, P], i32)
        block_row = sb("block_row", [1, CHUNK_TILES], i32)
        dst_loc = sb("dst_loc", [P, CHUNK_TILES])
        dst_col = sb("dst_col", [P, CHUNK_TILES])
        to_col = sb("to_col", [P, CHUNK_TILES])
        w_col = sb("w_col", [P, CHUNK_TILES])
        src_col = sb("src_col", [P, CHUNK_TILES], i32)
        rel_col = sb("rel_col", [P, CHUNK_TILES], i32)
        key_col = sb("key_col", [P, CHUNK_TILES], i32)

        iota_f = sb("iota_f", [P, WINDOWS * WINDOW])
        ident = sb("ident", [P, P])
        ones = sb("ones", [P, P])
        zeros = sb("zeros", [P, BANK], bf16)

        w_gate = sb("w_gate", [D + 1, 4 * D])
        w1l_sb = sb("w1l_sb", [D, HID])
        w1r_sb = sb("w1r_sb", [D, HID])
        b1_sb = sb("b1_sb", [HID, 1])
        w2_sb = sb("w2_sb", [HID, 2 * D])
        b2_sb = sb("b2_sb", [1, 2 * D])
        rel_sb = sb("rel_sb", [D, R, D])

        X = sb("X", [P, BLOCKS, D])
        H = sb("H", [P, BLOCKS, D])
        dev = sb("dev", [P, BLOCKS, D])
        sq = sb("sq", [P, BLOCKS, D])
        row_sum = sb("row_sum", [P, BLOCKS])
        mean = sb("mean", [P, BLOCKS])
        sq_sum = sb("sq_sum", [P, BLOCKS])
        var = sb("var", [P, BLOCKS])
        std = sb("std", [P, BLOCKS])
        rstd = sb("rstd", [P, BLOCKS])
        degree = sb("degree", [P, BLOCKS])
        rdeg = sb("rdeg", [P, BLOCKS])
        proj = sb("proj", [P, BLOCKS, 4 * D])
        agg = sb("agg", [P, BLOCKS, D])
        own = proj[:, :, 0:2 * D]
        rel_out = proj[:, :, :].rearrange("p b n -> p (b n)")[:, 0:4 * R * D].rearrange("p (k n) -> p k n", k=4)
        light = sq
        hT = sb("hT", [D + 1, NPAD])

        idx_slot = sb("idx_slot", [P, SLOTS, GROUP], i32)
        key_slot = sb("key_slot", [P, SLOTS, GROUP], i32)
        qv_rows = sb("qv_rows", [P, SLOTS, GROUP, 2 * D])
        hot = sb("hot", [P, SLOTS, GROUP, WINDOW])
        iota_i = hot[:, :, :, :].rearrange("p s j w -> p (s j w)")[:, 0:WINDOWS * WINDOW].bitcast(i32)

        acc = ctx.enter_context(nc.psum_tensor("acc", [P, ACC_BANKS * BANK], f32))
        work = ctx.enter_context(nc.psum_tensor("work", [P, 4, BANK], f32))
        acc_blocks = acc[:, 0:BLOCKS * D].rearrange("p (b d) -> p b d", d=D)

        edges_in, weights_in, x_in = sem("edges_in"), sem("weights_in"), sem("x_in")
        pool_const, row_const = sem("pool_const"), sem("row_const")
        vec_step = sem("vec_step")
        edge_fields = sem("edge_fields")
        edge_turned = sem("edge_turned")
        edge_copied = sem("edge_copied")
        counted = sem("counted")
        flag_ready = sem("flag_ready")
        block_stored, block_loaded = sem("block_stored"), sem("block_loaded")
        var_ready, std_ready = sem("var_ready"), sem("std_ready")
        node_ready = sem("node_ready")
        turned = sem("turned")
        turned_copied = sem("turned_copied")
        product = sem("product")
        product_copied = sem("product_copied")
        table_ready = sem("table_ready")
        table_stored = sem("table_stored")
        rel_stored = [sem(f"rel_stored{k}") for k in range(4)]
        acc_free = sem("acc_free")
        acc_ready = sem("acc_ready")
        slot_open = [sem(f"slot_open{s}") for s in range(SLOTS)]
        idx_ready = [sem(f"idx_ready{s}") for s in range(SLOTS)]
        gathered = [sem(f"gathered{s}") for s in range(SLOTS)]
        hot_ready = [sem(f"hot_ready{s}") for s in range(SLOTS)]
        gate_in = [sem(f"gate_in{s}") for s in range(SLOTS)]
        gate_out = [sem(f"gate_out{s}") for s in range(SLOTS)]
        all_idx, all_rows, all_hot, all_open = sem("all_idx"), sem("all_rows"), sem("all_hot"), sem("all_open")
        light_idx, light_rows, light_hot, light_open = sem("light_idx"), sem("light_rows"), sem("light_hot"), sem("light_open")
        all_gate_in, all_gate_out = sem("all_gate_in"), sem("all_gate_out")
        slot_taken = sem("slot_taken")
        out_stored = sem("out_stored")

        TURNS = ITERS + 1
        EDGE_FIELDS = 7
        FIELD_BANKS = -(-CHUNKS // PER_BANK)
        FULL_CHUNKS = E // (P * P)
        MORE = (E - FULL_CHUNKS * P * P) // P
        REST = E - FULL_CHUNKS * P * P - MORE * P
        GATE_BANKS = -(-BLOCKS // 2)
        SAGE1_BANKS = TCHUNKS
        SAGE2_BANKS = -(-BLOCKS // 4)
        REL_BANKS = 2 * BLOCKS

        with nc.allow_non_contiguous_dma(reason="bias columns"):
            block = ctx.enter_context(nc.Block())

            @block.sync
            def _(sp):
                sp.wait_ge(pool_const, 4)
                for raw, field in ((dst_raw, dst), (src_raw, src), (et_raw, etype), (w_raw, weight)):
                    a, b = FULL_CHUNKS * P * P, FULL_CHUNKS * P * P + MORE * P
                    sp.dma_start(raw[:, 0:FULL_CHUNKS, :],
                                 field[0:a].rearrange("(j q p) -> q j p", q=P, p=P)).then_inc(edges_in, 16)
                    sp.dma_start(raw[0:MORE, FULL_CHUNKS, :],
                                 field[a:b].rearrange("(q p) -> q p", p=P)).then_inc(edges_in, 16)
                    sp.dma_start(raw[MORE:MORE + 1, FULL_CHUNKS, 0:REST],
                                 field[b:E].rearrange("(a n) -> a n", a=1)).then_inc(edges_in, 16)
                sp.wait_ge(edge_copied, EDGE_FIELDS * FIELD_BANKS + 1)
                sp.dma_start(block_d, block_t[:, :]).then_inc(block_stored, 16)
                sp.wait_ge(block_stored, 16)
                sp.dma_start(block_row[:, :], block_d.rearrange("(a j) p -> a (j p)", a=1)).then_inc(block_loaded, 16)

                def by_block(tab):
                    return tab.rearrange("(b p) d -> p b d", p=P)

                sp.wait_ge(table_ready, 1)
                sp.dma_start(by_block(key_tab), proj[:, :, 0:D]).then_inc(table_stored, 16)
                sp.dma_start(by_block(qv_tab), proj[:, :, D:3 * D]).then_inc(table_stored, 16)
                sp.wait_ge(table_ready, 2)
                sp.dma_start(by_block(node_tab[1]), H[:, :, :]).then_inc(table_stored, 16)
                sp.wait_ge(table_ready, 3)
                sp.dma_start(by_block(node_tab[2]), own[:, :, 0:D]).then_inc(table_stored, 16)
                before = GATE_BANKS + SAGE1_BANKS + SAGE2_BANKS
                for b in range(BLOCKS):
                    sp.wait_ge(product_copied, before + 2 * b + 2)
                    sp.dma_start(rel_tab[b * P * R:(b + 1) * P * R, :].rearrange("(p r) d -> p (r d)", r=R),
                                 rel_out[:, b % 4, :]).then_inc(rel_stored[b % 4], 16)
                for p, ready in ((4, H), (5, agg), (6, agg)):
                    sp.wait_ge(table_ready, p)
                    sp.dma_start(by_block(node_tab[p]), ready[:, :, :]).then_inc(table_stored, 16)
                sp.wait_ge(table_ready, 7)
                sp.dma_start(out[0:FULL_BLOCKS * P, :].rearrange("(b p) d -> p b d", p=P),
                             X[:, 0:FULL_BLOCKS, :]).then_inc(out_stored, 16)
                sp.dma_start(out[FULL_BLOCKS * P:N, :], X[0:TAIL, FULL_BLOCKS, :]).then_inc(out_stored, 16)
                sp.wait_ge(out_stored, 32)

            @block.gpsimd
            def _(pool):
                pool.memset(dst_raw[:, :, :], int(FAR)).then_inc(pool_const, 1)
                pool.memset(src_raw[:, :, :], 0).then_inc(pool_const, 1)
                pool.memset(et_raw[:, :, :], 0).then_inc(pool_const, 1)
                pool.memset(w_raw[:, :, :], 0.0).then_inc(pool_const, 1)
                pool.memset(X[:, FULL_BLOCKS, :], 0.0).then_inc(pool_const, 1)
                pool.memset(ident[:, :], 0.0).then_inc(pool_const, 1)
                pool.memset(ones[:, :], 1.0).then_inc(pool_const, 1)
                pool.memset(zeros[:, :], 0.0).then_inc(pool_const, 1)
                pool.iota(iota_i[:, :], pattern=[[1, WINDOWS * WINDOW]], base=0, channel_multiplier=0).then_inc(pool_const, 1)
                pool.wait_ge(pool_const, 9)
                pool.affine_select(out=ident[:, :], in_=ident[:, :], compare_op=ALU.not_equal, fill=1.0,
                                   base=0, pattern=[[-1, P]], channel_multiplier=1).then_inc(pool_const, 1)
                pool.wait_ge(flag_ready, 1)
                far = pool.value_load(spread[0:1, 0:1], min_val=0, max_val=1)
                for p in range(PASSES):
                    tab = (qv_tab, node_tab[1], node_tab[2], rel_tab, node_tab[4], node_tab[5], node_tab[6])[p]
                    dest = qv_rows if p == 0 else rows
                    stored = (32, 48, 64, 64, 80, 96, 112)[p]
                    pool.wait_ge(table_stored, stored)
                    if p == 3:
                        for k in range(4):
                            pool.wait_ge(rel_stored[k], 16 * len(range(k, BLOCKS, 4)))
                    def near():
                        with pool.Fori(0, ITERS) as i:
                            for s in range(SLOTS):
                                pool.wait_ge(idx_ready[s], i + (p * ITERS + 1))
                                pool.sem_inc(slot_taken, 1)
                                for j in range(GROUP):
                                    pool.indirect_dma_start(
                                        dest[:, s, j, :], None, tab,
                                        bass.IndirectOffsetOnAxis(ap=idx_slot[:, s, j:j + 1], axis=0)).then_inc(gathered[s], 16)
                                    if p == 0:
                                        pool.indirect_dma_start(
                                            key_rows[:, s, j, :], None, key_tab,
                                            bass.IndirectOffsetOnAxis(ap=key_slot[:, s, j:j + 1], axis=0)).then_inc(gathered[s], 16)
                    def everywhere(idx_sem, rows_sem, q):
                        with pool.Fori(0, TILES) as t:
                            pool.wait_ge(idx_sem, t + (q * TILES + 1))
                            pool.sem_inc(slot_taken, 1)
                            pool.indirect_dma_start(
                                dest[:, 0, 0, :], None, tab,
                                bass.IndirectOffsetOnAxis(ap=idx_slot[:, 0, 0:1], axis=0)).then_inc(rows_sem, 16)
                            if p == 0:
                                pool.indirect_dma_start(
                                    key_rows[:, 0, 0, :], None, key_tab,
                                    bass.IndirectOffsetOnAxis(ap=key_slot[:, 0, 0:1], axis=0)).then_inc(rows_sem, 16)

                    if p >= 4:
                        everywhere(light_idx, light_rows, p - 4)
                        continue
                    with pool.If(far == 0):
                        near()
                    with pool.Else():
                        everywhere(all_idx, all_rows, p)

            @block.vector
            def _(vec):
                n = 0

                def after():
                    vec.wait_ge(vec_step, n)

                vec.memset(hT[D:D + 1, :], 1.0).then_inc(row_const, 1)
                vec.memset(b2_sb[:, :], 0.0).then_inc(row_const, 1)
                vec.wait_ge(pool_const, 9)
                vec.tensor_copy(iota_f[:, :], iota_i[:, :]).then_inc(vec_step, 1)
                vec.wait_ge(edges_in, 12 * 16)
                vec.tensor_copy(dst_f[:, :, :], dst_raw[:, :, :]).then_inc(vec_step, 1)
                vec.tensor_copy(src_f[:, :, :], src_raw[:, :, :]).then_inc(vec_step, 1)
                vec.tensor_copy(et_f[:, :, :], et_raw[:, :, :]).then_inc(vec_step, 1)
                n = 4
                after()
                vec.tensor_reduce(tile_min[:, :], dst_f[:, :, :], AX.X, ALU.min).then_inc(vec_step, 1)
                vec.scalar_tensor_tensor(rel_f[:, :, :], src_f[:, :, :], float(R), et_f[:, :, :], ALU.mult, ALU.add).then_inc(vec_step, 1)
                vec.tensor_scalar(key_f[:, :, :], dst_f[:, :, :], float(N - 1), None, ALU.min).then_inc(vec_step, 1)
                n = 7
                after()
                vec.tensor_scalar(min_i[:, :], tile_min[:, :], float(N - 1), None, ALU.min).then_inc(vec_step, 1)
                n = 8
                after()
                vec.tensor_scalar(block_i[:, :], min_i[:, :], 7, None, ALU.arith_shift_right).then_inc(vec_step, 1)
                n = 9
                after()
                vec.tensor_copy(block_f[:, :], block_i[:, :]).then_inc(vec_step, 1)
                n = 10
                after()
                vec.tensor_scalar(base_f[:, :], block_f[:, :], float(P), None, ALU.mult).then_inc(vec_step, 1)
                n = 11
                after()
                vec.tensor_tensor(loc_f[:, :, :], dst_f[:, :, :],
                                  base_f[:, :].unsqueeze(2).to_broadcast([P, CHUNKS, P]), ALU.subtract).then_inc(vec_step, 1)
                n = 12
                after()
                vec.tensor_scalar(inside[:, :, :], loc_f[:, :, :], float(WINDOW), None, ALU.is_lt).then_inc(vec_step, 1)
                n = 13
                after()
                vec.tensor_reduce(n_inside[:, :], inside[:, :, :].rearrange("p a b -> p (a b)"), AX.X, ALU.add).then_inc(edge_fields, 1)
                vec.wait_ge(counted, 1)
                vec.tensor_scalar(spread[:, :], work[0:1, 3, 0:1], float(E), None, ALU.is_lt).then_inc(flag_ready, 1)
                m = 0
                for field in (dst_loc, dst_col, w_col, to_col, src_col, rel_col, key_col):
                    for c in range(FIELD_BANKS):
                        vec.wait_ge(edge_turned, m + 1)
                        size = min(PER_BANK, CHUNKS - PER_BANK * c) * P
                        vec.tensor_copy(field[:, c * BANK:c * BANK + size], work[:, m % 3, 0:size]).then_inc(edge_copied, 1)
                        m += 1
                vec.wait_ge(edge_turned, m + 1)
                vec.tensor_copy(block_t[:, :], work[0:CHUNKS, m % 3, 0:P]).then_inc(edge_copied, 1)
                vec.wait_ge(edge_copied, m + 1)
                vec.wait_ge(flag_ready, 1)
                far = vec.value_load(spread[0:1, 0:1], min_val=0, max_val=1)

                def layernorm(nth):
                    nonlocal n
                    wide = [P, BLOCKS, D]
                    after()
                    vec.tensor_reduce(row_sum[:, :], X[:, :, :], AX.X, ALU.add).then_inc(vec_step, 1)
                    n += 1
                    after()
                    vec.tensor_scalar(mean[:, :], row_sum[:, :], 1.0 / D, None, ALU.mult).then_inc(vec_step, 1)
                    n += 1
                    after()
                    vec.tensor_tensor(dev[:, :, :], X[:, :, :], mean[:, :].unsqueeze(2).to_broadcast(wide), ALU.subtract).then_inc(vec_step, 1)
                    n += 1
                    after()
                    vec.tensor_tensor(sq[:, :, :], dev[:, :, :], dev[:, :, :], ALU.mult).then_inc(vec_step, 1)
                    n += 1
                    after()
                    vec.tensor_reduce(sq_sum[:, :], sq[:, :, :], AX.X, ALU.add).then_inc(vec_step, 1)
                    n += 1
                    after()
                    vec.tensor_scalar(var[:, :], sq_sum[:, :], 1.0 / D, EPS, ALU.mult, ALU.add).then_inc(var_ready, 1)
                    vec.wait_ge(std_ready, nth)
                    vec.reciprocal(rstd[:, :], std[:, :]).then_inc(vec_step, 1)
                    n += 1
                    after()
                    vec.tensor_tensor(dev[:, :, :], dev[:, :, :], rstd[:, :].unsqueeze(2).to_broadcast(wide), ALU.mult).then_inc(vec_step, 1)
                    n += 1
                    after()

                def edge_pass(p):
                    idx = rel_col if p == 3 else key_col if p >= 4 else src_col

                    def near():
                        with vec.Fori(0, ITERS) as i:
                            for s in range(SLOTS):
                                t = i * (SLOTS * GROUP) + s * GROUP
                                vec.wait_ge(slot_open[s], i + (p * TURNS + 1))
                                if p == 0:
                                    vec.tensor_copy(key_slot[:, s, :], key_col[:, bass.ds(t, GROUP)])
                                vec.tensor_copy(idx_slot[:, s, :], idx[:, bass.ds(t, GROUP)]).then_inc(idx_ready[s], 1)
                            for s in range(SLOTS):
                                for j in range(GROUP):
                                    t = i * (SLOTS * GROUP) + (s * GROUP + j)
                                    last = vec.tensor_scalar(
                                        hot[:, s, j, :], iota_f[:, 0:WINDOW], dst_loc[:, bass.ds(t, 1)],
                                        1.0, ALU.is_equal, ALU.mult)
                                if p:
                                    last.then_inc(hot_ready[s], 1)
                                if p == 0:
                                    vec.wait_ge(gathered[s], i * (2 * 16 * GROUP) + 2 * 16 * GROUP)
                                    vec.tensor_tensor(key_rows[:, s, :, :], key_rows[:, s, :, :],
                                                      qv_rows[:, s, :, 0:D], ALU.add).then_inc(gate_in[s], 1)
                                    vec.wait_ge(gate_out[s], i + 1)
                                    vec.tensor_tensor(rows[:, s, :, :], key_rows[:, s, :, :],
                                                      qv_rows[:, s, :, D:2 * D], ALU.mult).then_inc(hot_ready[s], 1)
                    def everywhere(q, open_sem, idx_sem, rows_sem, hot_sem):
                        to = to_col if p >= 4 else dst_col
                        wide = hot[:, :, :, :].rearrange("p s j w -> p (s j w)")[:, 0:WINDOWS * WINDOW]
                        with vec.Fori(0, TILES) as t:
                            vec.wait_ge(open_sem, t + (q * (TILES + 1) + 1))
                            if p == 0:
                                vec.tensor_copy(key_slot[:, 0, 0:1], key_col[:, bass.ds(t, 1)])
                            vec.tensor_copy(idx_slot[:, 0, 0:1], idx[:, bass.ds(t, 1)]).then_inc(idx_sem, 1)
                            last = vec.tensor_scalar(wide, iota_f[:, :], to[:, bass.ds(t, 1)],
                                                     w_col[:, bass.ds(t, 1)] if p >= 4 else 1.0, ALU.is_equal, ALU.mult)
                            if p:
                                last.then_inc(hot_sem, 1)
                            if p == 0:
                                vec.wait_ge(rows_sem, t * 32 + 32)
                                vec.tensor_tensor(key_rows[:, 0, 0, :], key_rows[:, 0, 0, :],
                                                  qv_rows[:, 0, 0, 0:D], ALU.add).then_inc(all_gate_in, 1)
                                vec.wait_ge(all_gate_out, t + 1)
                                vec.tensor_tensor(rows[:, 0, 0, :], key_rows[:, 0, 0, :],
                                                  qv_rows[:, 0, 0, D:2 * D], ALU.mult).then_inc(hot_sem, 1)

                    if p >= 4:
                        everywhere(p - 4, light_open, light_idx, light_rows, light_hot)
                    else:
                        with vec.If(far == 0):
                            near()
                        with vec.Else():
                            everywhere(p, all_open, all_idx, all_rows, all_hot)

                wide = [P, BLOCKS, D]
                vec.wait_ge(x_in, 32)
                layernorm(1)
                vec.tensor_scalar(H[:, :, :], dev[:, :, :], 0.0, None, ALU.max).then_inc(node_ready, 1)
                edge_pass(0)
                vec.wait_ge(product_copied, GATE_BANKS)
                vec.tensor_tensor(X[:, :, :], X[:, :, :], proj[:, :, 3 * D:4 * D], ALU.add).then_inc(vec_step, 1)
                n += 1
                vec.wait_ge(acc_ready, 1)
                after()
                vec.tensor_tensor(X[:, :, :], X[:, :, :], acc_blocks, ALU.add).then_inc(vec_step, 1)
                vec.tensor_scalar(degree[:, :], acc[:, CNT0:CNT0 + BLOCKS], 1.0, None, ALU.max).then_inc(vec_step, 1)
                n += 2
                after()
                vec.reciprocal(rdeg[:, :], degree[:, :]).then_inc(acc_free, 1)
                layernorm(2)
                vec.wait_ge(turned, TCHUNKS)
                vec.tensor_scalar(H[:, :, :], dev[:, :, :], 0.0, None, ALU.max).then_inc(node_ready, 1)
                vec.wait_ge(node_ready, 2)
                edge_pass(1)
                vec.wait_ge(acc_ready, 2)
                vec.wait_ge(acc_free, 1)
                vec.tensor_tensor(agg[:, :, :], acc_blocks, rdeg[:, :].unsqueeze(2).to_broadcast(wide), ALU.mult).then_inc(acc_free, 1)
                edge_pass(2)
                vec.wait_ge(acc_ready, 3)
                vec.wait_ge(turned, 3 * TCHUNKS)
                vec.tensor_tensor(agg[:, :, :], acc_blocks, rdeg[:, :].unsqueeze(2).to_broadcast(wide), ALU.mult).then_inc(acc_free, 1)
                vec.wait_ge(product_copied, GATE_BANKS + SAGE1_BANKS + SAGE2_BANKS)
                vec.wait_ge(acc_free, 3)
                vec.tensor_tensor(agg[:, :, :], agg[:, :, :], own[:, :, D:2 * D], ALU.add).then_inc(vec_step, 1)
                n += 1
                after()
                vec.scalar_tensor_tensor(X[:, :, :], agg[:, :, :], 0.0, X[:, :, :], ALU.max, ALU.add).then_inc(vec_step, 1)
                n += 1
                layernorm(3)
                vec.wait_ge(table_stored, 48)
                vec.tensor_scalar(H[:, :, :], dev[:, :, :], 0.0, None, ALU.max).then_inc(node_ready, 1)
                edge_pass(3)
                vec.wait_ge(acc_ready, 4)
                vec.tensor_tensor(X[:, :, :], X[:, :, :], acc_blocks, ALU.add).then_inc(vec_step, 1)
                n += 1
                after()
                layernorm(4)
                vec.wait_ge(turned, 4 * TCHUNKS)
                vec.tensor_scalar(H[:, :, :], dev[:, :, :], 0.0, None, ALU.max).then_inc(table_ready, 1)
                vec.wait_ge(table_ready, 4)
                vec.tensor_copy(light[:, :, :], H[:, :, :]).then_inc(acc_free, 1)
                edge_pass(4)
                vec.wait_ge(acc_ready, 5)
                vec.tensor_copy(agg[:, :, :], acc_blocks).then_inc(table_ready, 1)
                vec.wait_ge(acc_free, 4)
                vec.tensor_tensor(light[:, :, :], light[:, :, :], acc_blocks, ALU.add).then_inc(acc_free, 1)
                edge_pass(5)
                vec.wait_ge(acc_ready, 6)
                vec.wait_ge(table_stored, 96)
                vec.tensor_copy(agg[:, :, :], acc_blocks).then_inc(table_ready, 1)
                vec.wait_ge(acc_free, 5)
                vec.tensor_tensor(light[:, :, :], light[:, :, :], acc_blocks, ALU.add).then_inc(acc_free, 1)
                edge_pass(6)
                vec.wait_ge(acc_ready, 7)
                vec.wait_ge(acc_free, 6)
                vec.tensor_tensor(light[:, :, :], light[:, :, :], acc_blocks, ALU.add).then_inc(vec_step, 1)
                n += 1
                after()
                vec.scalar_tensor_tensor(X[:, :, :], light[:, :, :], 0.25, X[:, :, :], ALU.mult, ALU.add).then_inc(table_ready, 1)

            @block.scalar
            def _(act):
                act.wait_ge(pool_const, 5)
                act.dma_start(X[:, 0:FULL_BLOCKS, :],
                              x[0:FULL_BLOCKS * P, :].rearrange("(b p) d -> p b d", p=P)).then_inc(x_in, 16)
                act.dma_start(X[0:TAIL, FULL_BLOCKS, :], x[FULL_BLOCKS * P:N, :]).then_inc(x_in, 16)
                for k, (w, b) in enumerate(((w_key, b_key), (w_query, b_query), (w_value, b_value), (w_skip, b_skip))):
                    act.dma_start(w_gate[0:D, k * D:(k + 1) * D], w).then_inc(weights_in, 16)
                    act.dma_start(w_gate[D:D + 1, k * D:(k + 1) * D], b.rearrange("(a n) -> a n", a=1)).then_inc(weights_in, 16)
                act.dma_start(w1l_sb[:, :], w1_l).then_inc(weights_in, 16)
                act.dma_start(w1r_sb[:, :], w1_r).then_inc(weights_in, 16)
                act.dma_start(b1_sb[:, :], b1.rearrange("(n a) -> n a", a=1)).then_inc(weights_in, 16)
                act.dma_start(w2_sb[:, 0:D], w2_l).then_inc(weights_in, 16)
                act.dma_start(w2_sb[:, D:2 * D], w2_r).then_inc(weights_in, 16)
                act.wait_ge(row_const, 2)
                act.dma_start(b2_sb[:, D:2 * D], b2.rearrange("(a n) -> a n", a=1)).then_inc(weights_in, 16)
                act.dma_start(rel_sb[:, :, :], w_rel.rearrange("r i o -> i r o")).then_inc(weights_in, 16)
                act.wait_ge(flag_ready, 1)
                far = act.value_load(spread[0:1, 0:1], min_val=0, max_val=1)

                def root(nth):
                    act.wait_ge(var_ready, nth)
                    act.activation(std[:, :], var[:, :], ACT.Sqrt).then_inc(std_ready, 1)

                def take_turned(nth, to):
                    for c in range(TCHUNKS):
                        size = min(PER_BANK, BLOCKS - PER_BANK * c) * P
                        act.wait_ge(turned, nth * TCHUNKS + c + 1)
                        act.activation(to[0:D, c * BANK:c * BANK + size], work[0:D, c % 4, 0:size], ACT.Copy).then_inc(turned_copied, 1)

                root(1)
                take_turned(0, hT)
                for c in range(GATE_BANKS):
                    k = min(2, BLOCKS - 2 * c)
                    act.wait_ge(product, c + 1)
                    act.activation(proj[:, 2 * c:2 * c + k, :], work[:, c % 4, 0:k * 4 * D].rearrange("p (b n) -> p b n", b=k),
                                   ACT.Copy).then_inc(product_copied, 1)
                act.wait_ge(product_copied, GATE_BANKS)
                act.sem_inc(table_ready, 1)
                with act.If(far == 0):
                    with act.Fori(0, ITERS) as i:
                        for s in range(SLOTS):
                            act.wait_ge(gate_in[s], i + 1)
                            act.activation(key_rows[:, s, :, :], key_rows[:, s, :, :], ACT.Sigmoid).then_inc(gate_out[s], 1)
                with act.Else():
                    with act.Fori(0, TILES) as t:
                        act.wait_ge(all_gate_in, t + 1)
                        act.activation(key_rows[:, 0, 0, :], key_rows[:, 0, 0, :], ACT.Sigmoid).then_inc(all_gate_out, 1)
                root(2)
                act.wait_ge(node_ready, 2)
                act.sem_inc(table_ready, 1)
                take_turned(1, hT)
                take_turned(2, mT)
                done = GATE_BANKS
                for c in range(SAGE1_BANKS):
                    size = min(BANK, NPAD - BANK * c)
                    act.wait_ge(product, done + c + 1)
                    act.activation(gT[:, c * BANK:c * BANK + size], work[:, c % 4, 0:size], ACT.Relu,
                                   bias=b1_sb[:, 0:1]).then_inc(product_copied, 1)
                done += SAGE1_BANKS
                for c in range(SAGE2_BANKS):
                    k = min(4, BLOCKS - 4 * c)
                    act.wait_ge(product, done + c + 1)
                    act.activation(own[:, 4 * c:4 * c + k, :], work[:, c % 4, 0:k * 2 * D].rearrange("p (b n) -> p b n", b=k),
                                   ACT.Copy).then_inc(product_copied, 1)
                done += SAGE2_BANKS
                act.wait_ge(product_copied, done)
                act.sem_inc(table_ready, 1)
                root(3)
                take_turned(3, hT)
                for c in range(REL_BANKS):
                    b = c // 2
                    if b >= 4:
                        act.wait_ge(rel_stored[b % 4], 16 * (b // 4))
                    act.wait_ge(product, done + c + 1)
                    act.activation(rel_out[:, b % 4, (c % 2) * BANK:(c % 2 + 1) * BANK], work[:, c % 4, :], ACT.Copy).then_inc(product_copied, 1)
                root(4)

            @block.tensor
            def _(pe):
                pe.wait_ge(pool_const, 10)
                pe.wait_ge(row_const, 2)
                pe.wait_ge(edge_fields, 1)
                pe.matmul(work[0:1, 3, 0:1], n_inside[:, :], ones[:, 0:1], start=True, stop=True).then_inc(counted, 1)
                m = 0
                for field in (loc_f, dst_f, w_raw, src_f, src_f, rel_f, key_f):
                    for c in range(FIELD_BANKS):
                        if m >= 3:
                            pe.wait_ge(edge_copied, m - 2)
                        k = min(PER_BANK, CHUNKS - PER_BANK * c)
                        for j in range(k):
                            last = pe.transpose(work[:, m % 3, j * P:(j + 1) * P], field[:, PER_BANK * c + j, :], ident[:, :])
                        last.then_inc(edge_turned, 1)
                        m += 1
                pe.wait_ge(edge_copied, m - 2)
                pe.transpose(work[0:CHUNKS, m % 3, 0:P], block_f[:, :], ident[:, :]).then_inc(edge_turned, 1)
                pe.wait_ge(edge_copied, m + 1)
                pe.wait_ge(block_loaded, 16)
                pe.wait_ge(flag_ready, 1)
                far = pe.value_load(spread[0:1, 0:1], min_val=0, max_val=1)

                def turn(nth, of):
                    for c in range(TCHUNKS):
                        k = min(PER_BANK, BLOCKS - PER_BANK * c)
                        if c >= 4:
                            pe.wait_ge(turned_copied, nth * TCHUNKS + c - 3)
                        for j in range(k):
                            last = pe.transpose(work[0:D, c % 4, j * P:(j + 1) * P], of[:, PER_BANK * c + j, :], ident[:, :])
                        last.then_inc(turned, 1)

                def edge_pass(p):
                    if p:
                        pe.wait_ge(acc_free, p)
                    for k in range(ACC_BANKS):
                        last = pe.matmul(acc[:, k * BANK:(k + 1) * BANK], zeros[:, 0:P], zeros[:, :], start=True, stop=True, skip_group_check=True)
                        if k < SLOTS:
                            last.then_inc(slot_open[k], 1)
                        else:
                            last.then_inc(light_open if p >= 4 else all_open, 1)

                    def add(lhs, rhs, at):
                        return pe.matmul(acc[:, at], lhs, rhs, start=False, stop=True, skip_group_check=True)

                    def near():
                        with pe.Fori(0, ITERS) as i:
                            for s in range(SLOTS):
                                pe.wait_ge(hot_ready[s], i + (p * ITERS + 1))
                                if p:
                                    pe.wait_ge(gathered[s], i * (16 * GROUP) + (p + 1) * ITERS * 16 * GROUP + 16 * GROUP)
                                for j in range(GROUP):
                                    t = i * (SLOTS * GROUP) + (s * GROUP + j)
                                    b = pe.value_load(block_row[0:1, bass.ds(t, 1)], min_val=0, max_val=BLOCKS - 1)
                                    for h in range(2):
                                        lhs = hot[:, s, j, h * P:(h + 1) * P]
                                        last = add(lhs, rows[:, s, j, :], bass.ds(b * D + h * D, D))
                                        if p == 0:
                                            last = add(lhs, ones[:, 0:1], bass.ds(b + (CNT0 + h), 1))
                                last.then_inc(slot_open[s], 1)

                    def everywhere(q, open_sem, rows_sem, hot_sem):
                        wide = hot[:, :, :, :].rearrange("p s j w -> p (s j w)")
                        with pe.Fori(0, TILES) as t:
                            pe.wait_ge(hot_sem, t + (q * TILES + 1))
                            if p:
                                pe.wait_ge(rows_sem, t * 16 + ((q if p >= 4 else q + 1) * TILES * 16 + 16))
                            for b in range(2 * WINDOWS):
                                lhs = wide[:, b * P:(b + 1) * P]
                                last = add(lhs, rows[:, 0, 0, :], slice(b * D, (b + 1) * D))
                                if p == 0:
                                    last = add(lhs, ones[:, 0:1], slice(CNT0 + b, CNT0 + b + 1))
                            last.then_inc(open_sem, 1)

                    if p >= 4:
                        everywhere(p - 4, light_open, light_rows, light_hot)
                    else:
                        with pe.If(far == 0):
                            near()
                        with pe.Else():
                            everywhere(p, all_open, all_rows, all_hot)
                    pe.matmul(work[:, 0, 0:1], zeros[:, 0:P], zeros[:, 0:1], start=True, stop=True).then_inc(acc_ready, 1)

                pe.wait_ge(weights_in, 15 * 16)
                pe.wait_ge(node_ready, 1)
                turn(0, H)
                pe.wait_ge(turned_copied, TCHUNKS)
                for c in range(GATE_BANKS):
                    if c >= 4:
                        pe.wait_ge(product_copied, c - 3)
                    for k in range(min(2, BLOCKS - 2 * c)):
                        b = 2 * c + k
                        last = pe.matmul(work[:, c % 4, k * 4 * D:(k + 1) * 4 * D], hT[:, b * P:(b + 1) * P], w_gate[:, :], start=True, stop=True)
                    last.then_inc(product, 1)
                pe.wait_ge(product_copied, GATE_BANKS)
                edge_pass(0)
                pe.wait_ge(node_ready, 2)
                turn(1, H)
                pe.wait_ge(turned_copied, 2 * TCHUNKS)
                edge_pass(1)
                pe.wait_ge(acc_free, 2)
                turn(2, agg)
                pe.wait_ge(turned_copied, 3 * TCHUNKS)
                done = GATE_BANKS
                for c in range(SAGE1_BANKS):
                    if c >= 4:
                        pe.wait_ge(product_copied, done + c - 3)
                    size = min(BANK, NPAD - BANK * c)
                    pe.matmul(work[:, c % 4, 0:size], w1l_sb[:, :], mT[:, c * BANK:c * BANK + size], start=True, stop=False)
                    pe.matmul(work[:, c % 4, 0:size], w1r_sb[:, :], hT[0:D, c * BANK:c * BANK + size], start=False, stop=True).then_inc(product, 1)
                done += SAGE1_BANKS
                pe.wait_ge(product_copied, done)
                for c in range(SAGE2_BANKS):
                    if c >= 4:
                        pe.wait_ge(product_copied, done + c - 3)
                    for k in range(min(4, BLOCKS - 4 * c)):
                        b = 4 * c + k
                        at = work[:, c % 4, k * 2 * D:(k + 1) * 2 * D]
                        pe.matmul(at, gT[:, b * P:(b + 1) * P], w2_sb[:, :], start=True, stop=False)
                        last = pe.matmul(at, ones[0:1, :], b2_sb[:, :], start=False, stop=True)
                    last.then_inc(product, 1)
                done += SAGE2_BANKS
                pe.wait_ge(product_copied, done)
                edge_pass(2)
                pe.wait_ge(node_ready, 3)
                turn(3, H)
                pe.wait_ge(turned_copied, 4 * TCHUNKS)
                for c in range(REL_BANKS):
                    if c >= 4:
                        pe.wait_ge(product_copied, done + c - 3)
                    pe.matmul(work[:, c % 4, :], hT[0:D, (c // 2) * P:(c // 2 + 1) * P],
                              rel_sb[:, (c % 2) * (R // 2):(c % 2 + 1) * (R // 2), :].rearrange("i r o -> i (r o)"),
                              start=True, stop=True).then_inc(product, 1)
                done += REL_BANKS
                pe.wait_ge(product_copied, done)
                edge_pass(3)
                edge_pass(4)
                edge_pass(5)
                edge_pass(6)


_INS = ['x', 'src', 'dst', 'edge_type_16', 'edge_weight', 'L0_gnn_W_key', 'L0_gnn_b_key', 'L0_gnn_W_query', 'L0_gnn_b_query',
        'L0_gnn_W_value', 'L0_gnn_b_value', 'L0_gnn_W_skip', 'L0_gnn_b_skip', 'L1_gnn_W1_l', 'L1_gnn_b1', 'L1_gnn_W1_r',
        'L1_gnn_W2_l', 'L1_gnn_b2', 'L1_gnn_W2_r', 'L2_gnn_weight']


def kernel(**inputs):
    import numpy as _np
    import concourse.bacc as _bacc
    from concourse import mybir as _mybir
    from concourse.bass_utils import run_bass_kernel_spmd as _run

    nc = _bacc.Bacc("TRN2", target_bir_lowering=False, num_devices=1)
    arrays, args = {}, []
    for name in _INS:
        a = _np.ascontiguousarray(inputs[name])
        arrays[f"in_{name}_dram"] = a
        args.append(nc.dram_tensor(f"in_{name}_dram", a.shape, _mybir.dt.from_np(a.dtype), kind="ExternalInput").ap())
    args.append(nc.dram_tensor("out_0_dram", (N, D), _mybir.dt.float32, kind="ExternalOutput").ap())
    build(nc, *args)
    r = _run(nc, [arrays], core_ids=[0])
    return r.results[0]["out_0_dram"]
```

```python
from contextlib import ExitStack

import concourse.bass as bass
from concourse import mybir

N = 3125
D = 64
HID = 128
E = 103125
R = 16
P = 128
BLOCKS = -(-N // P)
FULL_BLOCKS = N // P
TAIL = N - FULL_BLOCKS * P
NPAD = BLOCKS * P
GROUP = 8
SLOTS = 3
TILES = -(-E // (P * GROUP * SLOTS)) * GROUP * SLOTS
ITERS = TILES // (GROUP * SLOTS)
CHUNKS = -(-TILES // P)
COLS = CHUNKS * P
WINDOW = 2 * P
WINDOWS = (BLOCKS + 1) // 2
BANK = 512
ACC_BANKS = 4
CNT0 = 2 * WINDOWS * D
PER_BANK = BANK // P
TCHUNKS = -(-BLOCKS // PER_BANK)
EPS = 1e-5
PASSES = 7
FAR = 4096.0
STRIPE = 16
STRIPES = P // STRIPE
ALL_STRIPES = BLOCKS * STRIPES
CAP = 6
PAIRS = STRIPE * BLOCKS
RING = 5
ROUNDS = BLOCKS // RING


def build(nc, x, src, dst, etype, weight, w_key, b_key, w_query, b_query, w_value, b_value,
          w_skip, b_skip, w1_l, b1, w1_r, w2_l, b2, w2_r, w_rel, out):
    f32 = mybir.dt.float32
    f16 = mybir.dt.float16
    i32 = mybir.dt.int32
    bf16 = mybir.dt.bfloat16
    ALU = mybir.AluOpType
    ACT = mybir.ActivationFunctionType
    AX = mybir.AxisListType

    ctx = ExitStack()
    with ctx:
        def sb(name, shape, dt=f32):
            return ctx.enter_context(nc.sbuf_tensor(name, shape, dt))

        def sem(name):
            return ctx.enter_context(nc.semaphore(name))

        def dram(name, shape, dt=f32):
            return nc.dram_tensor(name, shape, dt, kind="Internal").ap()

        key_tab = dram("key_tab", [NPAD, D])
        qv_tab = dram("qv_tab", [NPAD, 2 * D])
        rel_tab = dram("rel_tab", [NPAD * R, D])
        node_tab = [dram(f"node_tab{p}", [NPAD, D]) for p in range(PASSES)]
        ends_d = dram("ends_d", [2, CHUNKS, P])
        count_d = dram("count_d", [BLOCKS, P, NPAD], bf16)
        light_d = dram("light_d", [BLOCKS, P, NPAD])

        dst_loc = sb("dst_loc", [P, COLS])
        pair_col = sb("pair_col", [P, COLS])
        low_col = sb("low_col", [P, COLS])
        w_plane = [sb(f"w_plane{k}", [P, COLS]) for k in range(3)]
        src_col = sb("src_col", [P, COLS], i32)
        rel_col = sb("rel_col", [P, COLS], i32)
        key_col = sb("key_col", [P, COLS], i32)
        block_row = sb("block_row", [1, COLS], i32)
        first_tile = sb("first_tile", [1, ALL_STRIPES], i32)
        spread = sb("spread", [1, 1], i32)

        iota_w = sb("iota_w", [P, WINDOW])
        iota_h = sb("iota_h", [P, PAIRS], f16)
        stripe0 = sb("stripe0", [P, ALL_STRIPES + 1])
        pair0 = sb("pair0", [P, ALL_STRIPES])
        ident = sb("ident", [P, P])
        ones = sb("ones", [P, P])
        zeros = sb("zeros", [P, BANK], bf16)

        w_gate = sb("w_gate", [D + 1, 4 * D])
        w1l_sb = sb("w1l_sb", [D, HID])
        w1r_sb = sb("w1r_sb", [D, HID])
        b1_sb = sb("b1_sb", [HID, 1])
        w2_sb = sb("w2_sb", [HID, 2 * D])
        b2_sb = sb("b2_sb", [1, 2 * D])
        rel_sb = sb("rel_sb", [D, R, D])

        X = sb("X", [P, BLOCKS, D])
        H = sb("H", [P, BLOCKS, D])
        dev = sb("dev", [P, BLOCKS, D])
        sq = sb("sq", [P, BLOCKS, D])
        row_sum = sb("row_sum", [P, BLOCKS])
        mean = sb("mean", [P, BLOCKS])
        sq_sum = sb("sq_sum", [P, BLOCKS])
        var = sb("var", [P, BLOCKS])
        std = sb("std", [P, BLOCKS])
        rstd = sb("rstd", [P, BLOCKS])
        degree = sb("degree", [P, BLOCKS])
        rdeg = sb("rdeg", [P, BLOCKS])
        agg = sb("agg", [P, BLOCKS, D])
        light = sq
        planes = sb("planes", [P, BLOCKS, 3, D], bf16)
        hT = sb("hT", [D + 1, NPAD])

        ROWS = SLOTS * GROUP * D
        DESK = BLOCKS * 4 * D
        desk = sb("desk", [P, DESK + 4 * ROWS])
        proj = desk[:, 0:DESK].rearrange("p (b n) -> p b n", b=BLOCKS)
        own = proj[:, :, 0:2 * D]
        rel_out = desk[:, 0:4 * R * D].rearrange("p (k n) -> p k n", k=4)
        hot = desk[:, 0:SLOTS * GROUP * WINDOW].rearrange("p (s j w) -> p s j w", s=SLOTS, w=WINDOW)
        rows = desk[:, DESK:DESK + ROWS].rearrange("p (s j d) -> p s j d", s=SLOTS, d=D)
        key_rows = desk[:, DESK + ROWS:DESK + 2 * ROWS].rearrange("p (s j d) -> p s j d", s=SLOTS, d=D)
        qv_rows = desk[:, DESK + 2 * ROWS:DESK + 4 * ROWS].rearrange("p (s j d) -> p s j d", s=SLOTS, d=2 * D)
        gT = desk[:, DESK + ROWS:DESK + ROWS + NPAD]
        dst_raw, src_raw, et_raw = (desk[:, k * COLS:(k + 1) * COLS].bitcast(i32).rearrange("p (j q) -> p j q", q=P) for k in range(3))
        w_raw, dst_f, src_f, rel_f, real_f = (desk[:, k * COLS:(k + 1) * COLS].rearrange("p (j q) -> p j q", q=P) for k in range(3, 8))
        A = 8 * COLS
        BELOW = ALL_STRIPES + 1
        below = [desk[:, A + k * BELOW * CHUNKS:A + (k + 1) * BELOW * CHUNKS].rearrange("p (g j) -> p g j", j=CHUNKS) for k in range(2)]
        A += 2 * BELOW * CHUNKS
        ends_row = desk[0:1, A:A + 2 * COLS].rearrange("a (k t) -> a k t", k=2)
        A += 2 * COLS
        ends_t = desk[0:CHUNKS, A:A + 2 * P].rearrange("p (k q) -> p k q", k=2)
        A += 2 * P
        n_below = desk[:, A:A + 2 * BELOW].rearrange("p (k g) -> p k g", k=2)
        assert A + 2 * BELOW <= DESK + 4 * ROWS
        high_i, first_i = (desk[:, k * COLS:(k + 1) * COLS].bitcast(i32) for k in range(2))
        high_f, first_f, left_f, left2_f = (desk[:, k * COLS:(k + 1) * COLS] for k in range(2, 6))
        w_half = [desk[:, (6 * COLS + k * COLS // 2):(6 * COLS + (k + 1) * COLS // 2)].bitcast(bf16) for k in range(3)]
        check_row = desk[0:1, 8 * COLS:9 * COLS]
        check2_row = desk[0:1, 9 * COLS:10 * COLS]

        SPAN = WINDOWS * WINDOW
        A = 0
        BUILD = CAP * PAIRS + CAP * 4 * P + NPAD // 2 + 2 * NPAD
        arena = sb("arena", [P, BUILD])
        dst_col = arena[:, 0:COLS]
        to_col = arena[:, COLS:2 * COLS]
        w_col = arena[:, 2 * COLS:3 * COLS]
        iota_f = arena[:, 3 * COLS:3 * COLS + SPAN]
        wide_hot = arena[:, 3 * COLS + SPAN:3 * COLS + 2 * SPAN]
        assert 3 * COLS + 2 * SPAN <= BUILD - NPAD and RING * NPAD // 2 <= BUILD - NPAD
        mT = arena[0:D, BUILD - NPAD:BUILD]
        pair_hot = arena[:, 0:CAP * PAIRS].bitcast(bf16).rearrange("p (s k n) -> p s k n", s=2, k=CAP)
        A = CAP * PAIRS
        low_hot = arena[:, A:A + CAP * 4 * P].bitcast(bf16).rearrange("p (s k m n) -> p s k m n", s=2, k=CAP, m=4)
        A += CAP * 4 * P
        count_strip = arena[:, A:A + NPAD // 2].bitcast(bf16).rearrange("p (b n) -> p b n", n=P)
        A += NPAD // 2
        source_strip = arena[:, A:A + NPAD].rearrange("p (b n) -> p b n", n=P)
        A += NPAD
        light_strip = arena[:, A:A + NPAD]
        count_ring = arena[:, 0:RING * NPAD // 2].bitcast(bf16).rearrange("p (s b n) -> p s b n", s=RING, n=P)
        light_ring = [arena[:, s * NPAD:(s + 1) * NPAD] for s in range(3)] + [desk[:, s * NPAD:(s + 1) * NPAD] for s in range(2)]
        stage = sb("stage", [P, RING, D])
        rel_pair = sb("rel_pair", [P, 2, CAP])
        idx_slot = sb("idx_slot", [P, SLOTS, GROUP], i32)
        key_slot = sb("key_slot", [P, SLOTS, GROUP], i32)
        tile_min = sb("tile_min", [P, CHUNKS])
        tile_max = sb("tile_max", [P, CHUNKS])
        row_max = sb("row_max", [P, CHUNKS])
        found = sb("found", [1, 4])
        worst = sb("worst", [1, 1])
        row_i = agg[0:1, :, :].rearrange("a b d -> a (b d)")[:, 0:COLS].bitcast(i32)

        acc = ctx.enter_context(nc.psum_tensor("acc", [P, ACC_BANKS * BANK], f32))
        work = ctx.enter_context(nc.psum_tensor("work", [P, 4, BANK], f32))
        acc_blocks = acc[:, 0:BLOCKS * D].rearrange("p (b d) -> p b d", d=D)
        light_bank = [acc[:, k * BANK:(k + 1) * BANK] for k in range(ACC_BANKS)] + [work[:, k, :] for k in range(TCHUNKS - ACC_BANKS)]
        dense_bank = [work[:, k, :] for k in range(4)] + [acc[:, 0:BANK]]

        edges_in, weights_in, x_in = sem("edges_in"), sem("weights_in"), sem("x_in")
        pool_const, row_const = sem("pool_const"), sem("row_const")
        vec_step = sem("vec_step")
        fields_ready = sem("fields_ready")
        ends_ready = sem("ends_ready")
        edge_turned = sem("edge_turned")
        edge_copied = sem("edge_copied")
        below_ready, below_summed = sem("below_ready"), sem("below_summed")
        ends_stored, ends_loaded = sem("ends_stored"), sem("ends_loaded")
        setup_done = sem("setup_done")
        var_ready, std_ready = sem("var_ready"), sem("std_ready")
        node_ready = sem("node_ready")
        turned = sem("turned")
        turned_copied = sem("turned_copied")
        product = sem("product")
        product_copied = sem("product_copied")
        proj_taken = sem("proj_taken")
        table_ready, table_stored = sem("table_ready"), sem("table_stored")
        node_tab_ready, node_tab_stored = sem("node_tab_ready"), sem("node_tab_stored")
        rel_stored = [sem(f"rel_stored{k}") for k in range(4)]
        acc_free = sem("acc_free")
        acc_ready = sem("acc_ready")
        slot_open = [sem(f"slot_open{s}") for s in range(SLOTS)]
        idx_ready = [sem(f"idx_ready{s}") for s in range(SLOTS)]
        gathered = [sem(f"gathered{s}") for s in range(SLOTS)]
        hot_ready = [sem(f"hot_ready{s}") for s in range(SLOTS)]
        gate_in = [sem(f"gate_in{s}") for s in range(SLOTS)]
        gate_out = [sem(f"gate_out{s}") for s in range(SLOTS)]
        rel_ready = sem("rel_ready")
        low_ready = sem("low_ready")
        build_hot = [sem(f"build_hot{s}") for s in range(2)]
        weighted0, weighted = sem("weighted0"), sem("weighted")
        count_sum, count_taken = sem("count_sum"), sem("count_taken")
        source_sum, source_taken = sem("source_sum"), sem("source_taken")
        count_full, count_stored = sem("count_full"), sem("count_stored")
        source_full = sem("source_full")
        light_turned, light_taken = sem("light_turned"), sem("light_taken")
        light_full, light_stored = sem("light_full"), sem("light_stored")
        planes_ready = sem("planes_ready")
        count_in = [sem(f"count_in{s}") for s in range(RING)]
        dense_sum, dense_taken = sem("dense_sum"), sem("dense_taken")
        light_in = [sem(f"light_in{s}") for s in range(RING)]
        light_used = [sem(f"light_used{s}") for s in range(RING)]
        staged = sem("staged")
        light_sum, light_copied = sem("light_sum"), sem("light_copied")
        all_idx, all_hot, all_open = sem("all_idx"), sem("all_hot"), sem("all_open")
        all_rows = [sem(f"all_rows{p}") for p in range(PASSES)]
        all_gate_in, all_gate_out = sem("all_gate_in"), sem("all_gate_out")
        slot_taken, store_turn = sem("slot_taken"), sem("store_turn")
        out_stored = sem("out_stored")

        TURNS = ITERS + 1
        EDGE_FIELDS = 4
        FIELD_BANKS = -(-CHUNKS // PER_BANK)
        EDGE_BANKS = EDGE_FIELDS * FIELD_BANKS
        FULL_CHUNKS = E // (P * P)
        MORE = (E - FULL_CHUNKS * P * P) // P
        REST = E - FULL_CHUNKS * P * P - MORE * P
        GATE_BANKS = -(-BLOCKS // 2)
        SAGE1_BANKS = TCHUNKS
        SAGE2_BANKS = -(-BLOCKS // 4)
        REL_BANKS = 2 * BLOCKS
        SHARE = [(0, 1, 2), (3, 4, 5), (6, 7)]
        NEAR = {0: 0, 3: 1}

        block = ctx.enter_context(nc.Block())

        @block.sync
        def _(sp):
            sp.wait_ge(pool_const, 4)
            for raw, field in ((dst_raw, dst), (src_raw, src), (et_raw, etype), (w_raw, weight)):
                a, b = FULL_CHUNKS * P * P, FULL_CHUNKS * P * P + MORE * P
                sp.dma_start(raw[:, 0:FULL_CHUNKS, :],
                             field[0:a].rearrange("(j q p) -> q j p", q=P, p=P)).then_inc(edges_in, 16)
                sp.dma_start(raw[0:MORE, FULL_CHUNKS, :],
                             field[a:b].rearrange("(q p) -> q p", p=P)).then_inc(edges_in, 16)
                sp.dma_start(raw[MORE:MORE + 1, FULL_CHUNKS, 0:REST],
                             field[b:E].rearrange("(a n) -> a n", a=1)).then_inc(edges_in, 16)
            sp.wait_ge(edge_copied, EDGE_BANKS + 1)
            sp.dma_start(ends_d.rearrange("k j q -> j k q"), ends_t).then_inc(ends_stored, 16)
            sp.wait_ge(ends_stored, 16)
            sp.dma_start(ends_row.rearrange("a k t -> a (k t)"), ends_d.rearrange("(a k) j q -> a (k j q)", a=1)).then_inc(ends_loaded, 16)

            def by_block(tab):
                return tab.rearrange("(b p) d -> p b d", p=P)

            sp.wait_ge(table_ready, 1)
            sp.dma_start(by_block(key_tab), proj[:, :, 0:D]).then_inc(table_stored, 16)
            sp.dma_start(by_block(qv_tab), proj[:, :, D:3 * D]).then_inc(table_stored, 16)
            sp.wait_ge(setup_done, 1)
            far = sp.value_load(spread[0:1, 0:1], min_val=0, max_val=1)
            with sp.If(far == 0):
                sp.sem_inc(count_stored, 16)
                sp.sem_inc(light_stored, 16)
                with sp.Fori(0, BLOCKS) as b:
                    sp.wait_ge(count_full, b + 1)
                    sp.sem_inc(store_turn, 1)
                    sp.dma_start(count_d[bass.ds(b, 1), :, :].rearrange("a p n -> (a p) n"),
                                 count_strip.rearrange("p b n -> p (b n)")).then_inc(count_stored, 16)
                    sp.wait_ge(light_full, b + 1)
                    sp.sem_inc(store_turn, 1)
                    sp.dma_start(light_d[bass.ds(b, 1), :, :].rearrange("a p n -> (a p) n"), light_strip).then_inc(light_stored, 16)
                sp.wait_ge(count_stored, 16 * BLOCKS + 16)
                sp.wait_ge(light_stored, 16 * BLOCKS + 16)
                for d in range(2):
                    with sp.Fori(0, ROUNDS) as r:
                        for s in range(RING):
                            sp.wait_ge(dense_sum, r * RING + (d * BLOCKS + s + 1))
                            sp.sem_inc(store_turn, 1)
                            sp.dma_start(count_ring[:, s, :, :].rearrange("p b n -> p (b n)"),
                                         count_d[bass.ds(r * RING + s, 1), :, :].rearrange("a p n -> (a p) n")).then_inc(count_in[s], 16)
            with sp.Else():
                sp.wait_ge(node_tab_ready, 1)
                sp.dma_start(by_block(node_tab[1]), H[:, :, :]).then_inc(node_tab_stored, 16)
                sp.wait_ge(node_tab_ready, 2)
                sp.dma_start(by_block(node_tab[2]), own[:, :, 0:D]).then_inc(node_tab_stored, 16)
            before = GATE_BANKS + SAGE1_BANKS + SAGE2_BANKS
            for b in range(BLOCKS):
                sp.wait_ge(product_copied, before + 2 * b + 2)
                sp.dma_start(rel_tab[b * P * R:(b + 1) * P * R, :].rearrange("(p r) d -> p (r d)", r=R),
                             rel_out[:, b % 4, :]).then_inc(rel_stored[b % 4], 16)
            with sp.If(far == 0):
                sp.wait_ge(acc_ready, 3)
                for d in range(3):
                    with sp.Fori(0, ROUNDS) as r:
                        for s in range(RING):
                            if d == 0 and s == 3:
                                sp.wait_ge(acc_ready, 4)
                            sp.wait_ge(light_used[s], r + (d * ROUNDS + 1))
                            sp.sem_inc(store_turn, 1)
                            sp.dma_start(light_ring[s], light_d[bass.ds(r * RING + s, 1), :, :].rearrange("a p n -> (a p) n")).then_inc(light_in[s], 16)
            with sp.Else():
                for k, (p, ready) in enumerate(((4, H), (5, agg), (6, agg))):
                    sp.wait_ge(node_tab_ready, 3 + k)
                    sp.dma_start(by_block(node_tab[p]), ready[:, :, :]).then_inc(node_tab_stored, 16)
            sp.wait_ge(table_ready, 2)
            sp.dma_start(out[0:FULL_BLOCKS * P, :].rearrange("(b p) d -> p b d", p=P),
                         X[:, 0:FULL_BLOCKS, :]).then_inc(out_stored, 16)
            sp.dma_start(out[FULL_BLOCKS * P:N, :], X[0:TAIL, FULL_BLOCKS, :]).then_inc(out_stored, 16)
            sp.wait_ge(out_stored, 32)

        @block.gpsimd
        def _(pool):
            pool.memset(dst_raw, int(FAR)).then_inc(pool_const, 1)
            pool.memset(src_raw, 0).then_inc(pool_const, 1)
            pool.memset(et_raw, 0).then_inc(pool_const, 1)
            pool.memset(w_raw, 0.0).then_inc(pool_const, 1)
            pool.memset(X[:, FULL_BLOCKS, :], 0.0).then_inc(pool_const, 1)
            pool.memset(ident[:, :], 0.0).then_inc(pool_const, 1)
            pool.memset(ones[:, :], 1.0).then_inc(pool_const, 1)
            pool.memset(zeros[:, :], 0.0).then_inc(pool_const, 1)
            pool.wait_ge(pool_const, 8)
            pool.affine_select(out=ident[:, :], in_=ident[:, :], compare_op=ALU.not_equal, fill=1.0,
                               base=0, pattern=[[-1, P]], channel_multiplier=1).then_inc(pool_const, 1)
            for to, step in ((stripe0[:, :], STRIPE), (pair0[:, :], PAIRS), (iota_w[:, :], 1), (iota_h[:, :], 1), (iota_f, 1)):
                pool.iota(to, pattern=[[step, to.shape[1]]], base=0, channel_multiplier=0,
                          allow_small_or_imprecise_dtypes=True).then_inc(pool_const, 1)
            pool.wait_ge(setup_done, 1)
            far = pool.value_load(spread[0:1, 0:1], min_val=0, max_val=1)

            def gather(to, tab, idx, done):
                pool.indirect_dma_start(to, None, tab, bass.IndirectOffsetOnAxis(ap=idx, axis=0)).then_inc(done, 16)

            def near(p):
                q = NEAR[p]
                with pool.Fori(0, ITERS) as i:
                    for s in range(SLOTS):
                        pool.wait_ge(idx_ready[s], i + (q * TURNS + 1))
                        pool.wait_ge(slot_open[s], i + (q * TURNS + 1))
                        pool.sem_inc(slot_taken, 1)
                        for j in range(GROUP):
                            if p == 0:
                                gather(qv_rows[:, s, j, :], qv_tab, idx_slot[:, s, j:j + 1], gathered[s])
                                gather(key_rows[:, s, j, :], key_tab, key_slot[:, s, j:j + 1], gathered[s])
                            else:
                                gather(rows[:, s, j, :], rel_tab, idx_slot[:, s, j:j + 1], gathered[s])

            def everywhere(p):
                tab = (qv_tab, node_tab[1], node_tab[2], rel_tab, node_tab[4], node_tab[5], node_tab[6])[p]
                if p not in (0, 3):
                    pool.wait_ge(node_tab_stored, 16 * (1, 2, 3, 4, 5)[p - 1 if p < 3 else p - 2])
                with pool.Fori(0, TILES) as t:
                    pool.wait_ge(all_idx, t + (p * TILES + 1))
                    pool.sem_inc(slot_taken, 1)
                    gather((qv_rows if p == 0 else rows)[:, 0, 0, :], tab, idx_slot[:, 0, 0:1], all_rows[p])
                    if p == 0:
                        gather(key_rows[:, 0, 0, :], key_tab, key_slot[:, 0, 0:1], all_rows[p])

            pool.wait_ge(table_stored, 32)
            with pool.If(far == 0):
                near(0)
            with pool.Else():
                for p in range(3):
                    everywhere(p)
            for k in range(4):
                pool.wait_ge(rel_stored[k], 16 * len(range(k, BLOCKS, 4)))
            with pool.If(far == 0):
                near(3)
            with pool.Else():
                for p in range(3, PASSES):
                    everywhere(p)

        @block.vector
        def _(vec):
            n = 0

            def done(last):
                nonlocal n
                last.then_inc(vec_step, 1)
                n += 1
                vec.wait_ge(vec_step, n)

            vec.memset(hT[D:D + 1, :], 1.0).then_inc(row_const, 1)
            vec.memset(b2_sb[:, :], 0.0).then_inc(row_const, 1)
            vec.wait_ge(edges_in, 12 * 16)
            vec.tensor_copy(src_f, src_raw)
            vec.tensor_copy(rel_f, et_raw)
            done(vec.tensor_copy(dst_f, dst_raw))
            vec.scalar_tensor_tensor(rel_f, src_f, float(R), rel_f, ALU.mult, ALU.add).then_inc(fields_ready, 1)
            vec.tensor_reduce(tile_min[:, :], dst_f, AX.X, ALU.min)
            done(vec.scalar_tensor_tensor(real_f, dst_f, float(NPAD), dst_f, ALU.is_lt, ALU.mult))
            done(vec.tensor_reduce(row_max[:, :], real_f, AX.X, ALU.max))
            vec.tensor_tensor(tile_max[:, :], row_max[:, :], tile_min[:, :], ALU.max).then_inc(ends_ready, 1)
            vec.wait_ge(ends_ready, 1)
            vec.wait_ge(pool_const, 14)
            for k, end in enumerate((tile_max, tile_min)):
                vec.tensor_tensor(below[k], end[:, :].unsqueeze(1).to_broadcast([P, BELOW, CHUNKS]),
                                  stripe0[:, :].unsqueeze(2).to_broadcast([P, BELOW, CHUNKS]), ALU.is_lt).then_inc(vec_step, 1)
                n += 1
            vec.wait_ge(vec_step, n)
            for k in range(2):
                vec.tensor_reduce(n_below[:, k, :], below[k], AX.X, ALU.add).then_inc(below_ready, 1)
            m = 0
            for field in (dst_col, to_col, rel_col[:, :], w_col):
                for c in range(FIELD_BANKS):
                    vec.wait_ge(edge_turned, m + 1)
                    size = min(PER_BANK, CHUNKS - PER_BANK * c) * P
                    vec.tensor_copy(field[:, c * BANK:c * BANK + size], work[:, m % 3, 0:size]).then_inc(edge_copied, 1)
                    m += 1
            vec.wait_ge(edge_turned, m + 1)
            vec.tensor_copy(ends_t, work[0:CHUNKS, m % 3, 0:2 * P].rearrange("p (k q) -> p k q", k=2)).then_inc(edge_copied, 1)
            m += 1
            vec.wait_ge(edge_copied, m)
            vec.tensor_copy(src_col[:, :], to_col)
            done(vec.tensor_scalar(key_col[:, :], dst_col, float(N - 1), None, ALU.min))
            done(vec.tensor_scalar(high_i, src_col[:, :], 7, None, ALU.arith_shift_right))
            done(vec.tensor_copy(high_f, high_i))
            vec.scalar_tensor_tensor(low_col[:, :], high_f, -float(P), to_col, ALU.mult, ALU.add)
            vec.scalar_tensor_tensor(pair_col[:, :], dst_col, float(BLOCKS), high_f, ALU.mult, ALU.add)
            left = w_col
            for k in range(3):
                done(vec.tensor_copy(w_half[k], left))
                done(vec.tensor_copy(w_plane[k][:, :], w_half[k]))
                if k < 2:
                    rest = (left_f, left2_f)[k]
                    done(vec.tensor_tensor(rest, left, w_plane[k][:, :], ALU.subtract))
                    left = rest
            for c in range(2):
                vec.wait_ge(edge_turned, m + 1)
                vec.tensor_scalar(first_i[:, c * COLS // 2:(c + 1) * COLS // 2], work[:, m % 3, 0:COLS // 2],
                                  float(N - 1), None, ALU.min).then_inc(edge_copied, 1)
                m += 1
            vec.wait_ge(edge_copied, m)
            done(vec.tensor_scalar(high_i, first_i, 7, None, ALU.arith_shift_right))
            done(vec.tensor_copy(first_f, high_i))
            vec.scalar_tensor_tensor(dst_loc[:, :], first_f, -float(P), dst_col, ALU.mult, ALU.add)
            vec.wait_ge(ends_loaded, 16)
            done(vec.tensor_scalar(row_i[:, :], ends_row[:, 0, :], float(N - 1), None, ALU.min))
            done(vec.tensor_scalar(block_row[:, :], row_i[:, :], 7, None, ALU.arith_shift_right))
            vec.tensor_tensor(check_row[:, 0:COLS - 1], ends_row[:, 1, 0:COLS - 1], ends_row[:, 0, 1:COLS], ALU.subtract)
            done(vec.tensor_tensor(check2_row, ends_row[:, 1, :], ends_row[:, 0, :], ALU.subtract))
            done(vec.tensor_reduce(found[:, 0:1], check_row[:, 0:COLS - 1], AX.X, ALU.max))
            done(vec.tensor_scalar(check_row, check2_row, -float(P), None, ALU.add))
            done(vec.tensor_reduce(found[:, 1:2], check_row, AX.X, ALU.max))
            vec.tensor_scalar(check_row, ends_row[:, 0, :], float(NPAD), None, ALU.is_lt)
            done(vec.tensor_scalar(check2_row, check2_row, 1.0, None, ALU.is_lt))
            done(vec.tensor_tensor(check_row, check_row, check2_row, ALU.mult))
            done(vec.tensor_reduce(found[:, 2:3], check_row, AX.X, ALU.max))
            vec.wait_ge(below_summed, 1)
            sums = work[0:1, 3, 0:2 * BELOW].rearrange("a (k g) -> a k g", k=2)
            done(vec.tensor_copy(n_below[0:1, :, :], sums))
            vec.tensor_copy(first_tile[:, :], n_below[0:1, 0, 0:ALL_STRIPES])
            done(vec.tensor_tensor(check_row[:, 0:ALL_STRIPES], n_below[0:1, 1, 1:BELOW], n_below[0:1, 0, 0:ALL_STRIPES], ALU.subtract))
            done(vec.tensor_scalar(check_row[:, 0:ALL_STRIPES], check_row[:, 0:ALL_STRIPES], -float(CAP), None, ALU.add))
            done(vec.tensor_reduce(found[:, 3:4], check_row[:, 0:ALL_STRIPES], AX.X, ALU.max))
            done(vec.tensor_reduce(worst[:, :], found[:, :], AX.X, ALU.max))
            vec.tensor_scalar(spread[:, :], worst[:, :], 0.0, None, ALU.is_gt).then_inc(setup_done, 1)
            vec.wait_ge(setup_done, 1)
            far = vec.value_load(spread[0:1, 0:1], min_val=0, max_val=1)

            wide = [P, BLOCKS, D]

            def layernorm(nth):
                done(vec.tensor_reduce(row_sum[:, :], X[:, :, :], AX.X, ALU.add))
                done(vec.tensor_scalar(mean[:, :], row_sum[:, :], 1.0 / D, None, ALU.mult))
                done(vec.tensor_tensor(dev[:, :, :], X[:, :, :], mean[:, :].unsqueeze(2).to_broadcast(wide), ALU.subtract))
                done(vec.tensor_tensor(sq[:, :, :], dev[:, :, :], dev[:, :, :], ALU.mult))
                done(vec.tensor_reduce(sq_sum[:, :], sq[:, :, :], AX.X, ALU.add))
                vec.tensor_scalar(var[:, :], sq_sum[:, :], 1.0 / D, EPS, ALU.mult, ALU.add).then_inc(var_ready, 1)
                vec.wait_ge(std_ready, nth)
                done(vec.reciprocal(rstd[:, :], std[:, :]))
                done(vec.tensor_tensor(dev[:, :, :], dev[:, :, :], rstd[:, :].unsqueeze(2).to_broadcast(wide), ALU.mult))

            def split(of):
                done(vec.tensor_copy(planes[:, :, 0, :], of))
                done(vec.tensor_tensor(dev[:, :, :], of, planes[:, :, 0, :], ALU.subtract))
                done(vec.tensor_copy(planes[:, :, 1, :], dev[:, :, :]))
                done(vec.tensor_tensor(sq[:, :, :], dev[:, :, :], planes[:, :, 1, :], ALU.subtract))
                vec.tensor_copy(planes[:, :, 2, :], sq[:, :, :]).then_inc(planes_ready, 1)

            def build_stripe(b, k):
                g = b * STRIPES + k
                t = vec.value_load(first_tile[0:1, bass.ds(g, 1)], min_val=0, max_val=COLS - CAP)
                vec.wait_ge(source_sum, b * STRIPES + (k + 1))
                vec.tensor_scalar(rel_pair[:, k % 2, :], pair_col[:, bass.ds(t, CAP)], pair0[:, bass.ds(g, 1)], None,
                                  ALU.subtract).then_inc(rel_ready, 1)
                for c in range(CAP):
                    last = vec.tensor_scalar(low_hot[:, k % 2, c, 0, :], iota_h[:, 0:P], low_col[:, bass.ds(t + c, 1)], None, ALU.is_equal)
                last.then_inc(low_ready, 1)
                vec.wait_ge(rel_ready, b * STRIPES + (k + 1))
                for c in range(CAP):
                    last = vec.tensor_scalar(pair_hot[:, k % 2, c, :], iota_h[:, :], rel_pair[:, k % 2, c:c + 1], None, ALU.is_equal)
                last.then_inc(build_hot[k % 2], 1)
                vec.wait_ge(low_ready, b * STRIPES + (k + 1))
                vec.tensor_tensor(low_hot[:, k % 2, :, 1, :], low_hot[:, k % 2, :, 0, :],
                                  w_plane[0][:, bass.ds(t, CAP)].unsqueeze(2).to_broadcast([P, CAP, P]), ALU.mult).then_inc(weighted0, 1)

            def near(p):
                q = NEAR[p]
                idx = rel_col if p == 3 else src_col
                ROWS16 = 16 * GROUP * (2 if p == 0 else 1)
                before = q * 2 * ITERS * 16 * GROUP

                def indices(s, t):
                    if p == 0:
                        vec.tensor_copy(key_slot[:, s, :], key_col[:, bass.ds(t, GROUP)])
                    vec.tensor_copy(idx_slot[:, s, :], idx[:, bass.ds(t, GROUP)]).then_inc(idx_ready[s], 1)

                def iteration(i, build):
                    for s in range(SLOTS):
                        vec.wait_ge(slot_open[s], i + (q * TURNS + 1))
                        for j in range(GROUP):
                            t = i * (SLOTS * GROUP) + (s * GROUP + j)
                            last = vec.tensor_scalar(hot[:, s, j, :], iota_w[:, :], dst_loc[:, bass.ds(t, 1)], None, ALU.is_equal)
                        if p:
                            last.then_inc(hot_ready[s], 1)
                        vec.wait_ge(gathered[s], i * ROWS16 + (before + ROWS16))
                        indices(s, i * (SLOTS * GROUP) + (SLOTS * GROUP + s * GROUP))
                        if p == 0:
                            vec.tensor_tensor(key_rows[:, s, :, :], key_rows[:, s, :, :],
                                              qv_rows[:, s, :, 0:D], ALU.add).then_inc(gate_in[s], 1)
                        if build:
                            for k in SHARE[s]:
                                build_stripe(i, k)
                        if p == 0:
                            vec.wait_ge(gate_out[s], i + 1)
                            vec.tensor_tensor(rows[:, s, :, :], key_rows[:, s, :, :],
                                              qv_rows[:, s, :, D:2 * D], ALU.mult).then_inc(hot_ready[s], 1)

                for s in range(SLOTS):
                    indices(s, s * GROUP)
                if p == 0:
                    with vec.Fori(0, BLOCKS) as i:
                        iteration(i, True)
                    with vec.Fori(BLOCKS, ITERS) as i:
                        iteration(i, False)
                else:
                    with vec.Fori(0, ITERS) as i:
                        iteration(i, False)

            def everywhere(p):
                idx = rel_col if p == 3 else key_col if p >= 4 else src_col
                to = to_col if p >= 4 else dst_col
                with vec.Fori(0, TILES) as t:
                    vec.wait_ge(all_open, t + (p * (TILES + 1) + 1))
                    if p == 0:
                        vec.tensor_copy(key_slot[:, 0, 0:1], key_col[:, bass.ds(t, 1)])
                    vec.tensor_copy(idx_slot[:, 0, 0:1], idx[:, bass.ds(t, 1)]).then_inc(all_idx, 1)
                    last = vec.tensor_scalar(wide_hot, iota_f, to[:, bass.ds(t, 1)],
                                             w_col[:, bass.ds(t, 1)] if p >= 4 else 1.0, ALU.is_equal, ALU.mult)
                    if p:
                        last.then_inc(all_hot, 1)
                    if p == 0:
                        vec.wait_ge(all_rows[p], t * 32 + 32)
                        vec.tensor_tensor(key_rows[:, 0, 0, :], key_rows[:, 0, 0, :],
                                          qv_rows[:, 0, 0, 0:D], ALU.add).then_inc(all_gate_in, 1)
                        vec.wait_ge(all_gate_out, t + 1)
                        vec.tensor_tensor(rows[:, 0, 0, :], key_rows[:, 0, 0, :],
                                          qv_rows[:, 0, 0, D:2 * D], ALU.mult).then_inc(all_hot, 1)

            def means(d):
                with vec.If(far == 0):
                    with vec.Fori(0, ROUNDS) as r:
                        for s in range(RING):
                            vec.wait_ge(dense_sum, r * RING + (d * BLOCKS + s + 1 + RING))
                            vec.tensor_reduce(agg[:, bass.ds(r * RING + s, 1), :].rearrange("p a f -> p (a f)"),
                                              dense_bank[s][:, 0:3 * D].rearrange("p (k f) -> p f k", k=3),
                                              AX.X, ALU.add).then_inc(dense_taken, 1)
                    vec.wait_ge(dense_taken, (d + 1) * BLOCKS + RING)
                    vec.tensor_tensor(agg[:, :, :], agg[:, :, :], rdeg[:, :].unsqueeze(2).to_broadcast(wide), ALU.mult).then_inc(acc_free, 1)
                with vec.Else():
                    everywhere(1 + d)
                    vec.wait_ge(acc_ready, 2 + d)
                    vec.tensor_tensor(agg[:, :, :], acc_blocks, rdeg[:, :].unsqueeze(2).to_broadcast(wide), ALU.mult).then_inc(acc_free, 1)

            vec.wait_ge(x_in, 32)
            layernorm(1)
            vec.tensor_scalar(H[:, :, :], dev[:, :, :], 0.0, None, ALU.max).then_inc(node_ready, 1)
            vec.wait_ge(product_copied, GATE_BANKS)
            done(vec.tensor_tensor(X[:, :, :], X[:, :, :], proj[:, :, 3 * D:4 * D], ALU.add))
            vec.wait_ge(table_stored, 32)
            with vec.If(far == 0):
                near(0)
            with vec.Else():
                everywhere(0)
            vec.sem_inc(dense_taken, RING)
            vec.wait_ge(acc_ready, 1)
            vec.tensor_scalar(degree[:, :], acc[:, CNT0:CNT0 + BLOCKS], 1.0, None, ALU.max)
            done(vec.tensor_tensor(X[:, :, :], X[:, :, :], acc_blocks, ALU.add))
            vec.reciprocal(rdeg[:, :], degree[:, :]).then_inc(acc_free, 1)
            vec.wait_ge(acc_free, 1)

            layernorm(2)
            vec.wait_ge(turned, TCHUNKS)
            vec.tensor_scalar(H[:, :, :], dev[:, :, :], 0.0, None, ALU.max).then_inc(node_ready, 1)
            vec.wait_ge(node_ready, 2)
            vec.sem_inc(node_tab_ready, 1)
            split(H[:, :, :])
            means(0)
            vec.wait_ge(product_copied, GATE_BANKS + SAGE1_BANKS + SAGE2_BANKS)
            vec.sem_inc(node_tab_ready, 1)
            split(own[:, :, 0:D])
            vec.wait_ge(turned, 3 * TCHUNKS)
            means(1)
            vec.wait_ge(acc_free, 3)
            done(vec.tensor_tensor(agg[:, :, :], agg[:, :, :], own[:, :, D:2 * D], ALU.add))
            vec.sem_inc(proj_taken, 1)
            done(vec.scalar_tensor_tensor(X[:, :, :], agg[:, :, :], 0.0, X[:, :, :], ALU.max, ALU.add))

            layernorm(3)
            vec.tensor_scalar(H[:, :, :], dev[:, :, :], 0.0, None, ALU.max).then_inc(node_ready, 1)
            for k in range(4):
                vec.wait_ge(rel_stored[k], 16 * len(range(k, BLOCKS, 4)))
            with vec.If(far == 0):
                near(3)
            with vec.Else():
                everywhere(3)
            vec.wait_ge(acc_ready, 4)
            done(vec.tensor_tensor(X[:, :, :], X[:, :, :], acc_blocks, ALU.add))

            layernorm(4)
            vec.wait_ge(turned, 4 * TCHUNKS)
            done(vec.tensor_scalar(H[:, :, :], dev[:, :, :], 0.0, None, ALU.max))
            vec.sem_inc(node_tab_ready, 1)
            vec.tensor_copy(light[:, :, :], H[:, :, :]).then_inc(acc_free, 1)
            vec.wait_ge(acc_free, 4)
            for d in range(3):
                with vec.If(far == 0):
                    vec.wait_ge(light_sum, d + 1)
                    for c in range(ACC_BANKS):
                        vec.tensor_copy(hT[0:D, c * BANK:(c + 1) * BANK], light_bank[c][0:D, :]).then_inc(light_copied, 1)
                    vec.wait_ge(acc_ready, 5 + d)
                with vec.Else():
                    everywhere(4 + d)
                    vec.wait_ge(acc_ready, 5 + d)
                if d < 2:
                    done(vec.tensor_copy(agg[:, :, :], acc_blocks))
                    vec.sem_inc(node_tab_ready, 1)
                    vec.tensor_tensor(light[:, :, :], light[:, :, :], acc_blocks, ALU.add).then_inc(acc_free, 1)
                    vec.wait_ge(acc_free, 5 + d)
                else:
                    done(vec.tensor_tensor(light[:, :, :], light[:, :, :], acc_blocks, ALU.add))
            vec.scalar_tensor_tensor(X[:, :, :], light[:, :, :], 0.25, X[:, :, :], ALU.mult, ALU.add).then_inc(table_ready, 1)

        @block.scalar
        def _(act):
            act.wait_ge(pool_const, 5)
            act.dma_start(X[:, 0:FULL_BLOCKS, :],
                          x[0:FULL_BLOCKS * P, :].rearrange("(b p) d -> p b d", p=P)).then_inc(x_in, 16)
            act.dma_start(X[0:TAIL, FULL_BLOCKS, :], x[FULL_BLOCKS * P:N, :]).then_inc(x_in, 16)
            for k, (w, b) in enumerate(((w_key, b_key), (w_query, b_query), (w_value, b_value), (w_skip, b_skip))):
                act.dma_start(w_gate[0:D, k * D:(k + 1) * D], w).then_inc(weights_in, 16)
                act.dma_start(w_gate[D:D + 1, k * D:(k + 1) * D], b.rearrange("(a n) -> a n", a=1)).then_inc(weights_in, 16)
            act.dma_start(w1l_sb[:, :], w1_l).then_inc(weights_in, 16)
            act.dma_start(w1r_sb[:, :], w1_r).then_inc(weights_in, 16)
            act.dma_start(b1_sb[:, :], b1.rearrange("(n a) -> n a", a=1)).then_inc(weights_in, 16)
            act.dma_start(w2_sb[:, 0:D], w2_l).then_inc(weights_in, 16)
            act.dma_start(w2_sb[:, D:2 * D], w2_r).then_inc(weights_in, 16)
            act.wait_ge(row_const, 2)
            act.dma_start(b2_sb[:, D:2 * D], b2.rearrange("(a n) -> a n", a=1)).then_inc(weights_in, 16)
            act.dma_start(rel_sb[:, :, :], w_rel.rearrange("r i o -> i r o")).then_inc(weights_in, 16)
            act.wait_ge(setup_done, 1)
            far = act.value_load(spread[0:1, 0:1], min_val=0, max_val=1)

            def root(nth):
                act.wait_ge(var_ready, nth)
                act.activation(std[:, :], var[:, :], ACT.Sqrt).then_inc(std_ready, 1)

            def take_turned(nth, to):
                for c in range(TCHUNKS):
                    size = min(PER_BANK, BLOCKS - PER_BANK * c) * P
                    act.wait_ge(turned, nth * TCHUNKS + c + 1)
                    act.activation(to[0:D, c * BANK:c * BANK + size], work[0:D, c % 4, 0:size], ACT.Copy).then_inc(turned_copied, 1)

            def take_stripe(b, k):
                at = slice(k * STRIPE, (k + 1) * STRIPE)
                if k == 0:
                    act.wait_ge(count_stored, b * 16 + 16)
                act.wait_ge(count_sum, b * STRIPES + (k + 1))
                last = act.activation(count_strip[:, :, at], work[:, 0, 0:PAIRS].rearrange("p (n b) -> p b n", n=STRIPE), ACT.Copy)
                last.then_inc(count_taken, 1)
                act.wait_ge(source_sum, b * STRIPES + (k + 3))
                act.activation(source_strip[:, :, at], work[:, 1, 0:PAIRS].rearrange("p (n b) -> p b n", n=STRIPE),
                               ACT.Copy).then_inc(source_taken, 1)

            def weight_stripe(b, k):
                t = act.value_load(first_tile[0:1, bass.ds(b * STRIPES + k, 1)], min_val=0, max_val=COLS - CAP)
                act.wait_ge(low_ready, b * STRIPES + (k + 1))
                for c in range(CAP):
                    for m in range(1, 3):
                        last = act.activation(low_hot[:, k % 2, c, 1 + m, :], low_hot[:, k % 2, c, 0, :], ACT.Copy,
                                              scale=w_plane[m][:, bass.ds(t + c, 1)])
                last.then_inc(weighted, 1)

            root(1)
            take_turned(0, hT)
            for c in range(GATE_BANKS):
                k = min(2, BLOCKS - 2 * c)
                act.wait_ge(product, c + 1)
                act.activation(proj[:, 2 * c:2 * c + k, :], work[:, c % 4, 0:k * 4 * D].rearrange("p (b n) -> p b n", b=k),
                               ACT.Copy).then_inc(product_copied, 1)
            act.wait_ge(product_copied, GATE_BANKS)
            act.sem_inc(table_ready, 1)

            with act.If(far == 0):
                act.sem_inc(count_taken, 1)
                act.sem_inc(source_taken, 1)
                act.sem_inc(light_taken, 1)

                def iteration(i, build):
                    for s in range(SLOTS):
                        act.wait_ge(gate_in[s], i + 1)
                        act.activation(key_rows[:, s, :, :], key_rows[:, s, :, :], ACT.Sigmoid).then_inc(gate_out[s], 1)
                        if build:
                            for k in SHARE[s]:
                                weight_stripe(i, k)
                                if k:
                                    take_stripe(i, k - 1)
                    if build:
                        take_stripe(i, STRIPES - 1)
                        act.wait_ge(count_taken, i * STRIPES + (STRIPES + 1))
                        act.sem_inc(count_full, 1)
                        act.wait_ge(source_taken, i * STRIPES + (STRIPES + 1))
                        act.sem_inc(source_full, 1)
                        act.wait_ge(light_stored, i * 16 + 16)
                        for c in range(TCHUNKS):
                            size = min(PER_BANK, BLOCKS - PER_BANK * c) * P
                            act.wait_ge(light_turned, i * TCHUNKS + (c + 1))
                            act.activation(light_strip[:, c * BANK:c * BANK + size], work[:, 2 + c % 2, 0:size], ACT.Copy).then_inc(light_taken, 1)
                        act.wait_ge(light_taken, i * TCHUNKS + (TCHUNKS + 1))
                        act.sem_inc(light_full, 1)

                with act.Fori(0, BLOCKS) as i:
                    iteration(i, True)
                with act.Fori(BLOCKS, ITERS) as i:
                    iteration(i, False)
            with act.Else():
                with act.Fori(0, TILES) as t:
                    act.wait_ge(all_gate_in, t + 1)
                    act.activation(key_rows[:, 0, 0, :], key_rows[:, 0, 0, :], ACT.Sigmoid).then_inc(all_gate_out, 1)
            root(2)
            take_turned(1, hT)
            take_turned(2, mT)
            before = GATE_BANKS
            for c in range(SAGE1_BANKS):
                size = min(BANK, NPAD - BANK * c)
                act.wait_ge(product, before + c + 1)
                act.activation(gT[:, c * BANK:c * BANK + size], work[:, c % 4, 0:size], ACT.Relu,
                               bias=b1_sb[:, 0:1]).then_inc(product_copied, 1)
            before += SAGE1_BANKS
            for c in range(SAGE2_BANKS):
                k = min(4, BLOCKS - 4 * c)
                act.wait_ge(product, before + c + 1)
                act.activation(own[:, 4 * c:4 * c + k, :], work[:, c % 4, 0:k * 2 * D].rearrange("p (b n) -> p b n", b=k),
                               ACT.Copy).then_inc(product_copied, 1)
            before += SAGE2_BANKS
            root(3)
            take_turned(3, hT)
            act.wait_ge(proj_taken, 1)
            for c in range(REL_BANKS):
                b = c // 2
                if b >= 4:
                    act.wait_ge(rel_stored[b % 4], 16 * (b // 4))
                act.wait_ge(product, before + c + 1)
                act.activation(rel_out[:, b % 4, (c % 2) * BANK:(c % 2 + 1) * BANK], work[:, c % 4, :], ACT.Copy).then_inc(product_copied, 1)
            root(4)
            with act.If(far == 0):
                for d in range(3):
                    act.wait_ge(acc_free, 4 + d)
                    cur = H if d == 0 else agg
                    with act.Fori(0, ROUNDS) as r:
                        for s in range(RING):
                            act.wait_ge(light_used[s], r + (d * ROUNDS + 1))
                            act.activation(stage[:, s, :], cur[:, bass.ds(r * RING + s, 1), :].rearrange("p a f -> p (a f)"), ACT.Copy).then_inc(staged, 1)
                    act.wait_ge(light_sum, d + 1)
                    for c in range(ACC_BANKS, TCHUNKS):
                        size = min(BANK, NPAD - BANK * c)
                        act.activation(hT[0:D, c * BANK:c * BANK + size], light_bank[c][0:D, 0:size], ACT.Copy).then_inc(light_copied, 1)

        @block.tensor
        def _(pe):
            pe.wait_ge(pool_const, 14)
            pe.wait_ge(row_const, 2)
            pe.wait_ge(fields_ready, 1)
            m = 0
            for field in (dst_f, src_f, rel_f, w_raw):
                for c in range(FIELD_BANKS):
                    if m >= 3:
                        pe.wait_ge(edge_copied, m - 2)
                    for j in range(min(PER_BANK, CHUNKS - PER_BANK * c)):
                        last = pe.transpose(work[:, m % 3, j * P:(j + 1) * P], field[:, PER_BANK * c + j, :], ident[:, :])
                    last.then_inc(edge_turned, 1)
                    m += 1
                if m == 2 * FIELD_BANKS:
                    pe.wait_ge(below_ready, 2)
                    pe.matmul(work[0:1, 3, 0:2 * BELOW], ones[:, 0:1], n_below.rearrange("p k g -> p (k g)"), start=True, stop=True).then_inc(below_summed, 1)
            pe.wait_ge(edge_copied, m - 2)
            pe.wait_ge(ends_ready, 1)
            pe.transpose(work[0:CHUNKS, m % 3, 0:P], tile_min[:, :], ident[:, :])
            pe.transpose(work[0:CHUNKS, m % 3, P:2 * P], tile_max[:, :], ident[:, :]).then_inc(edge_turned, 1)
            m += 1
            pe.wait_ge(ends_loaded, 16)
            for c in range(2):
                pe.wait_ge(edge_copied, m - 2)
                pe.matmul(work[:, m % 3, 0:COLS // 2], ones[0:1, :], ends_row[:, 0, c * COLS // 2:(c + 1) * COLS // 2], start=True, stop=True).then_inc(edge_turned, 1)
                m += 1
            pe.wait_ge(edge_copied, m)
            pe.wait_ge(setup_done, 1)
            far = pe.value_load(spread[0:1, 0:1], min_val=0, max_val=1)

            def turn(nth, of):
                for c in range(TCHUNKS):
                    if c >= 4:
                        pe.wait_ge(turned_copied, nth * TCHUNKS + c - 3)
                    for j in range(min(PER_BANK, BLOCKS - PER_BANK * c)):
                        last = pe.transpose(work[0:D, c % 4, j * P:(j + 1) * P], of[:, PER_BANK * c + j, :], ident[:, :])
                    last.then_inc(turned, 1)

            def add(lhs, rhs, at):
                return pe.matmul(acc[:, at], lhs, rhs, start=False, stop=True, skip_group_check=True)

            def zero():
                for k in range(ACC_BANKS):
                    last = pe.matmul(acc[:, k * BANK:(k + 1) * BANK], zeros[:, 0:P], zeros[:, :], start=True, stop=True, skip_group_check=True)
                return last

            def finish():
                add(zeros[:, 0:P], zeros[:, 0:1], slice(ACC_BANKS * BANK - 1, ACC_BANKS * BANK)).then_inc(acc_ready, 1)

            def build_stripe(b, k):
                pe.wait_ge(build_hot[k % 2], b * (STRIPES // 2) + (k // 2 + 1))
                pe.wait_ge(count_taken, b * STRIPES + (k + 1))
                for c in range(CAP):
                    last = pe.matmul(work[:, 0, 0:PAIRS], low_hot[:, k % 2, c, 0, :], pair_hot[:, k % 2, c, :],
                                     start=c == 0, stop=c == CAP - 1)
                last.then_inc(count_sum, 1)
                pe.wait_ge(weighted0, b * STRIPES + (k + 1))
                pe.wait_ge(weighted, b * STRIPES + (k + 1))
                pe.wait_ge(source_taken, b * STRIPES + (k + 1))
                for c in range(CAP):
                    for m in range(3):
                        last = pe.matmul(work[:, 1, 0:PAIRS], low_hot[:, k % 2, c, 1 + m, :], pair_hot[:, k % 2, c, :],
                                         start=c + m == 0, stop=c == CAP - 1 and m == 2)
                last.then_inc(source_sum, 1)

            def near(p):
                q = NEAR[p]
                zero().then_inc(slot_open[0], 1)
                for s in range(1, SLOTS):
                    pe.sem_inc(slot_open[s], 1)

                def iteration(i, build):
                    for s in range(SLOTS):
                        if build:
                            for k in SHARE[s]:
                                build_stripe(i, k)
                        pe.wait_ge(hot_ready[s], i + (q * ITERS + 1))
                        if p:
                            pe.wait_ge(gathered[s], i * (16 * GROUP) + (2 * ITERS + 1) * 16 * GROUP)
                        for j in range(GROUP):
                            t = i * (SLOTS * GROUP) + (s * GROUP + j)
                            b = pe.value_load(block_row[0:1, bass.ds(t, 1)], min_val=0, max_val=BLOCKS - 1)
                            for h in range(2):
                                lhs = hot[:, s, j, h * P:(h + 1) * P]
                                last = add(lhs, rows[:, s, j, :], bass.ds(b * D + h * D, D))
                                if p == 0:
                                    last = add(lhs, ones[:, 0:1], bass.ds(b + (CNT0 + h), 1))
                        last.then_inc(slot_open[s], 1)
                    if build:
                        pe.wait_ge(source_full, i + 1)
                        for c in range(TCHUNKS):
                            if c != 1:
                                pe.wait_ge(light_taken, i * TCHUNKS + max(c, 1))
                            for j in range(min(PER_BANK, BLOCKS - PER_BANK * c)):
                                last = pe.transpose(work[:, 2 + c % 2, j * P:(j + 1) * P], source_strip[:, PER_BANK * c + j, :], ident[:, :])
                            last.then_inc(light_turned, 1)

                if p == 0:
                    pe.sem_inc(source_sum, 2)
                    pe.sem_inc(dense_sum, RING)
                    with pe.Fori(0, BLOCKS) as i:
                        iteration(i, True)
                    with pe.Fori(BLOCKS, ITERS) as i:
                        iteration(i, False)
                else:
                    for s in range(RING):
                        pe.sem_inc(light_used[s], 1)
                    with pe.Fori(0, ITERS) as i:
                        iteration(i, False)
                finish()

            def everywhere(p):
                zero().then_inc(all_open, 1)
                with pe.Fori(0, TILES) as t:
                    pe.wait_ge(all_hot, t + (p * TILES + 1))
                    if p:
                        pe.wait_ge(all_rows[p], t * 16 + 16)
                    for b in range(2 * WINDOWS):
                        lhs = wide_hot[:, b * P:(b + 1) * P]
                        last = add(lhs, rows[:, 0, 0, :], slice(b * D, (b + 1) * D))
                        if p == 0:
                            last = add(lhs, ones[:, 0:1], slice(CNT0 + b, CNT0 + b + 1))
                    last.then_inc(all_open, 1)
                finish()

            def counts(d):
                pe.wait_ge(planes_ready, d + 1)
                with pe.Fori(0, ROUNDS) as r:
                    for s in range(RING):
                        pe.wait_ge(count_in[s], r * 16 + (d * ROUNDS * 16 + 16))
                        pe.wait_ge(dense_taken, r * RING + (d * BLOCKS + s + 1))
                        for h in range(BLOCKS):
                            last = pe.matmul(dense_bank[s][:, 0:3 * D], count_ring[:, s, h, :],
                                             planes[:, h, :, :].rearrange("p k f -> p (k f)"), start=h == 0, stop=h == BLOCKS - 1)
                        last.then_inc(dense_sum, 1)
                finish()

            def lights(d):
                for bank in light_bank:
                    pe.matmul(bank, zeros[:, 0:P], zeros[:, :], start=True, stop=True, skip_group_check=True)
                with pe.Fori(0, ROUNDS) as r:
                    for s in range(RING):
                        pe.wait_ge(light_in[s], r * 16 + (d * ROUNDS * 16 + 16))
                        pe.wait_ge(staged, r * RING + (d * BLOCKS + s + 1))
                        for c in range(TCHUNKS):
                            size = min(BANK, NPAD - BANK * c)
                            last = pe.matmul(light_bank[c][0:D, 0:size], stage[:, s, :], light_ring[s][:, c * BANK:c * BANK + size],
                                             start=False, stop=True, skip_group_check=True)
                        last.then_inc(light_used[s], 1)
                pe.matmul(light_bank[-1][0:D, BANK - 1:BANK], zeros[:, 0:D], zeros[:, 0:1], start=False, stop=True,
                          skip_group_check=True).then_inc(light_sum, 1)
                pe.wait_ge(light_copied, (d + 1) * TCHUNKS)
                for b in range(BLOCKS):
                    pe.transpose(acc[:, b * D:(b + 1) * D], hT[0:D, b * P:(b + 1) * P], ident[0:D, 0:D])
                finish()

            pe.wait_ge(weights_in, 15 * 16)
            pe.wait_ge(node_ready, 1)
            turn(0, H)
            pe.wait_ge(turned_copied, TCHUNKS)
            for c in range(GATE_BANKS):
                if c >= 4:
                    pe.wait_ge(product_copied, c - 3)
                for k in range(min(2, BLOCKS - 2 * c)):
                    b = 2 * c + k
                    last = pe.matmul(work[:, c % 4, k * 4 * D:(k + 1) * 4 * D], hT[:, b * P:(b + 1) * P], w_gate[:, :], start=True, stop=True)
                last.then_inc(product, 1)
            pe.wait_ge(product_copied, GATE_BANKS)
            with pe.If(far == 0):
                near(0)
            with pe.Else():
                everywhere(0)

            pe.wait_ge(node_ready, 2)
            turn(1, H)
            pe.wait_ge(turned_copied, 2 * TCHUNKS)
            pe.wait_ge(acc_free, 1)
            with pe.If(far == 0):
                counts(0)
            with pe.Else():
                everywhere(1)
            pe.wait_ge(acc_free, 2)
            turn(2, agg)
            pe.wait_ge(turned_copied, 3 * TCHUNKS)
            before = GATE_BANKS
            for c in range(SAGE1_BANKS):
                if c >= 4:
                    pe.wait_ge(product_copied, before + c - 3)
                size = min(BANK, NPAD - BANK * c)
                pe.matmul(work[:, c % 4, 0:size], w1l_sb[:, :], mT[:, c * BANK:c * BANK + size], start=True, stop=False)
                pe.matmul(work[:, c % 4, 0:size], w1r_sb[:, :], hT[0:D, c * BANK:c * BANK + size], start=False, stop=True).then_inc(product, 1)
            before += SAGE1_BANKS
            pe.wait_ge(product_copied, before)
            for c in range(SAGE2_BANKS):
                if c >= 4:
                    pe.wait_ge(product_copied, before + c - 3)
                for k in range(min(4, BLOCKS - 4 * c)):
                    b = 4 * c + k
                    at = work[:, c % 4, k * 2 * D:(k + 1) * 2 * D]
                    pe.matmul(at, gT[:, b * P:(b + 1) * P], w2_sb[:, :], start=True, stop=False)
                    last = pe.matmul(at, ones[0:1, :], b2_sb[:, :], start=False, stop=True)
                last.then_inc(product, 1)
            before += SAGE2_BANKS
            pe.wait_ge(product_copied, before)
            with pe.If(far == 0):
                counts(1)
            with pe.Else():
                everywhere(2)

            pe.wait_ge(acc_free, 3)
            pe.wait_ge(node_ready, 3)
            turn(3, H)
            pe.wait_ge(turned_copied, 4 * TCHUNKS)
            for c in range(REL_BANKS):
                if c >= 4:
                    pe.wait_ge(product_copied, before + c - 3)
                pe.matmul(work[:, c % 4, :], hT[0:D, (c // 2) * P:(c // 2 + 1) * P],
                          rel_sb[:, (c % 2) * (R // 2):(c % 2 + 1) * (R // 2), :].rearrange("i r o -> i (r o)"),
                          start=True, stop=True).then_inc(product, 1)
            before += REL_BANKS
            pe.wait_ge(product_copied, before)
            with pe.If(far == 0):
                near(3)
            with pe.Else():
                everywhere(3)

            for d in range(3):
                pe.wait_ge(acc_free, 4 + d)
                with pe.If(far == 0):
                    lights(d)
                with pe.Else():
                    everywhere(4 + d)


_INS = ['x', 'src', 'dst', 'edge_type_16', 'edge_weight', 'L0_gnn_W_key', 'L0_gnn_b_key', 'L0_gnn_W_query', 'L0_gnn_b_query',
        'L0_gnn_W_value', 'L0_gnn_b_value', 'L0_gnn_W_skip', 'L0_gnn_b_skip', 'L1_gnn_W1_l', 'L1_gnn_b1', 'L1_gnn_W1_r',
        'L1_gnn_W2_l', 'L1_gnn_b2', 'L1_gnn_W2_r', 'L2_gnn_weight']


def kernel(**inputs):
    import numpy as _np
    import concourse.bacc as _bacc
    from concourse import mybir as _mybir
    from concourse.bass_utils import run_bass_kernel_spmd as _run

    nc = _bacc.Bacc("TRN2", target_bir_lowering=False, num_devices=1)
    arrays, args = {}, []
    for name in _INS:
        a = _np.ascontiguousarray(inputs[name])
        arrays[f"in_{name}_dram"] = a
        args.append(nc.dram_tensor(f"in_{name}_dram", a.shape, _mybir.dt.from_np(a.dtype), kind="ExternalInput").ap())
    args.append(nc.dram_tensor("out_0_dram", (N, D), _mybir.dt.float32, kind="ExternalOutput").ap())
    build(nc, *args)
    r = _run(nc, [arrays], core_ids=[0])
    return r.results[0]["out_0_dram"]
```

```python
from contextlib import ExitStack

import concourse.bass as bass
from concourse import mybir

N = 3125
D = 64
HID = 128
E = 103125
R = 16
P = 128
BLOCKS = -(-N // P)
FULL_BLOCKS = N // P
TAIL = N - FULL_BLOCKS * P
NPAD = BLOCKS * P
GROUP = 8
SLOTS = 3
TILES = -(-E // (P * GROUP * SLOTS)) * GROUP * SLOTS
ITERS = TILES // (GROUP * SLOTS)
CHUNKS = -(-TILES // P)
COLS = CHUNKS * P
ALL_BLOCKS = BLOCKS + 1
BANK = 512
ACC_BANKS = 4
FRAMES = ACC_BANKS * BANK // D
STEP = 100
TEAM = 4
FRAMED = GROUP // TEAM
STEP_SHIFT = 19
STEP_MUL = (1 << STEP_SHIFT) // STEP + 1
assert FRAMES * STEP >= N and N * STEP_MUL < 1 << 24
CNT0 = ALL_BLOCKS * D
PER_BANK = BANK // P
TCHUNKS = -(-BLOCKS // PER_BANK)
EPS = 1e-5
PASSES = 7
FAR = 4096.0
STRIPE = 16
STRIPES = P // STRIPE
ALL_STRIPES = BLOCKS * STRIPES
CAP = 6
PAIRS = STRIPE * BLOCKS
RING = 5
ROUNDS = BLOCKS // RING
PER_SLOT = 2
BLOCK_SLOTS = STRIPES // PER_SLOT
ROUND = SLOTS * BLOCK_SLOTS
ROUND_BLOCKS = ROUND // BLOCK_SLOTS
ROUND_ITERS = ROUND // SLOTS
EDGE_ROUNDS = ITERS // ROUND_ITERS
LAST = (ITERS - EDGE_ROUNDS * ROUND_ITERS) * SLOTS
assert EDGE_ROUNDS * ROUND_BLOCKS + 1 == BLOCKS and LAST > BLOCK_SLOTS


def build(nc, x, src, dst, etype, weight, w_key, b_key, w_query, b_query, w_value, b_value,
          w_skip, b_skip, w1_l, b1, w1_r, w2_l, b2, w2_r, w_rel, out):
    f32 = mybir.dt.float32
    f16 = mybir.dt.float16
    i32 = mybir.dt.int32
    bf16 = mybir.dt.bfloat16
    ALU = mybir.AluOpType
    ACT = mybir.ActivationFunctionType
    AX = mybir.AxisListType

    ctx = ExitStack()
    with ctx:
        def sb(name, shape, dt=f32):
            return ctx.enter_context(nc.sbuf_tensor(name, shape, dt))

        def sem(name):
            return ctx.enter_context(nc.semaphore(name))

        def dram(name, shape, dt=f32):
            return nc.dram_tensor(name, shape, dt, kind="Internal").ap()

        key_tab = dram("key_tab", [NPAD, D])
        qv_tab = dram("qv_tab", [NPAD, 2 * D])
        rel_tab = dram("rel_tab", [NPAD * R, D])
        node_tab = {p: dram(f"node_tab{p}", [NPAD, D]) for p in (1, 2, 4, 5, 6)}
        ends_d = dram("ends_d", [2, CHUNKS, P])
        count_d = dram("count_d", [BLOCKS, P, NPAD], bf16)
        loc_d = dram("loc_d", [COLS, P], f16)
        light_d = dram("light_d", [BLOCKS, P, NPAD])

        dst_loc = sb("dst_loc", [P, COLS])
        pair_col = sb("pair_col", [P, COLS])
        low_col = sb("low_col", [P, COLS])
        w_plane = [sb(f"w_plane{k}", [P, COLS]) for k in range(3)]
        src_col = sb("src_col", [P, COLS], i32)
        rel_col = sb("rel_col", [P, COLS], i32)
        key_col = sb("key_col", [P, COLS], i32)
        frame_row = sb("frame_row", [1, COLS], i32)
        first_tile = sb("first_tile", [1, ALL_STRIPES], i32)
        spread = sb("spread", [1, 1], i32)

        iota_w = sb("iota_w", [P, P])
        part = sb("part", [P, 1])
        iota_h = sb("iota_h", [P, PAIRS], f16)
        stripe0 = sb("stripe0", [P, ALL_STRIPES + 1])
        pair0 = sb("pair0", [P, ALL_STRIPES])
        shifts = sb("shifts", [P, 3 * P])
        ident = shifts[:, P:2 * P]
        ones = sb("ones", [P, P])
        zeros = sb("zeros", [P, BANK], bf16)

        w_gate = sb("w_gate", [D + 1, 4 * D])
        w1l_sb = sb("w1l_sb", [D, HID])
        w1r_sb = sb("w1r_sb", [D, HID])
        b1_sb = sb("b1_sb", [HID, 1])
        w2_sb = sb("w2_sb", [HID, 2 * D])
        b2_sb = sb("b2_sb", [1, 2 * D])
        rel_sb = sb("rel_sb", [D, R, D])

        X = sb("X", [P, BLOCKS, D])
        H = sb("H", [P, BLOCKS, D])
        dev = sb("dev", [P, BLOCKS, D])
        sq = sb("sq", [P, BLOCKS, D])
        row_sum = sb("row_sum", [P, BLOCKS])
        mean = sb("mean", [P, BLOCKS])
        sq_sum = sb("sq_sum", [P, BLOCKS])
        var = sb("var", [P, BLOCKS])
        std = sb("std", [P, BLOCKS])
        rstd = sb("rstd", [P, BLOCKS])
        degree = sb("degree", [P, BLOCKS])
        rdeg = sb("rdeg", [P, BLOCKS])
        keys = sb("keys", [P, FRAMES, D])
        agg = keys[:, 0:BLOCKS, :]
        light = sq
        planes = sb("planes", [P, BLOCKS, 3 * D + 2], bf16)
        plane = [planes[:, :, k * D:(k + 1) * D] for k in range(3)]
        hT = sb("hT", [D + 1, NPAD])

        ROWS = SLOTS * GROUP * D
        DESK = BLOCKS * 4 * D
        desk = sb("desk", [P, DESK + 4 * ROWS])
        proj = desk[:, 0:DESK].rearrange("p (b n) -> p b n", b=BLOCKS)
        own = proj[:, :, 0:2 * D]
        rel_out = desk[:, 0:4 * R * D].rearrange("p (k n) -> p k n", k=4)
        hot = desk[:, 0:SLOTS * GROUP * P].rearrange("p (s j w) -> p s j w", s=SLOTS, w=P)
        rows = desk[:, DESK:DESK + ROWS].rearrange("p (s j d) -> p s j d", s=SLOTS, d=D)
        key_rows = desk[:, DESK + ROWS:DESK + 2 * ROWS].rearrange("p (s j d) -> p s j d", s=SLOTS, d=D)
        qv_rows = desk[:, DESK + 2 * ROWS:DESK + 4 * ROWS].rearrange("p (s j d) -> p s j d", s=SLOTS, d=2 * D)
        gT = desk[:, DESK + ROWS:DESK + ROWS + NPAD]
        dst_raw, src_raw, et_raw = (desk[:, k * COLS:(k + 1) * COLS].bitcast(i32).rearrange("p (j q) -> p j q", q=P) for k in range(3))
        w_raw, dst_f, src_f, rel_f, real_f = (desk[:, k * COLS:(k + 1) * COLS].rearrange("p (j q) -> p j q", q=P) for k in range(3, 8))
        A = 8 * COLS
        BELOW = ALL_STRIPES + 1
        below = [desk[:, A + k * BELOW * CHUNKS:A + (k + 1) * BELOW * CHUNKS].rearrange("p (g j) -> p g j", j=CHUNKS) for k in range(2)]
        A += 2 * BELOW * CHUNKS
        ends_row = desk[0:1, A:A + 2 * COLS].rearrange("a (k t) -> a k t", k=2)
        A += 2 * COLS
        ends_t = desk[0:CHUNKS, A:A + 2 * P].rearrange("p (k q) -> p k q", k=2)
        A += 2 * P
        n_below = desk[:, A:A + 2 * BELOW].rearrange("p (k g) -> p k g", k=2)
        A += 2 * BELOW
        tile_min, tile_max, row_max = (desk[:, A + k * CHUNKS:A + (k + 1) * CHUNKS] for k in range(3))
        assert A + 3 * CHUNKS <= DESK + 4 * ROWS
        high_i, first_i = (desk[:, k * COLS:(k + 1) * COLS].bitcast(i32) for k in range(2))
        high_f, first_f, left_f, left2_f = (desk[:, k * COLS:(k + 1) * COLS] for k in range(2, 6))
        w_half = [desk[:, (6 * COLS + k * COLS // 2):(6 * COLS + (k + 1) * COLS // 2)].bitcast(bf16) for k in range(3)]
        check_row = desk[0:1, 8 * COLS:9 * COLS]
        check2_row = desk[0:1, 9 * COLS:10 * COLS]
        group_row = desk[0:1, 10 * COLS:11 * COLS]

        SPAN = ALL_BLOCKS * P
        A = 0
        BUILD = CAP * PAIRS + CAP * 4 * P + NPAD // 2 + 2 * NPAD
        arena = sb("arena", [P, BUILD])
        dst_col = arena[:, 0:COLS]
        to_col = arena[:, COLS:2 * COLS]
        w_col = arena[:, 2 * COLS:3 * COLS]
        iota_f = arena[:, 3 * COLS:3 * COLS + SPAN]
        wide_hot = arena[:, 3 * COLS + SPAN:3 * COLS + 2 * SPAN]
        assert 3 * COLS + 2 * SPAN <= BUILD - NPAD and RING * NPAD // 2 <= BUILD - NPAD
        mT = arena[0:D, BUILD - NPAD:BUILD]
        pair_hot = arena[:, 0:CAP * PAIRS].bitcast(bf16).rearrange("p (s k n) -> p s k n", s=2, k=CAP)
        A = CAP * PAIRS
        low_hot = arena[:, A:A + CAP * 4 * P].bitcast(bf16).rearrange("p (s k m n) -> p s k m n", s=2, k=CAP, m=4)
        pair_hots = [pair_hot[:, s, :, :] for s in range(2)] + [
            region.bitcast(bf16).rearrange("p (k n) -> p k n", k=CAP)
            for region in (desk[:, DESK + ROWS:DESK + ROWS + CAP * PAIRS // 2],
                           agg.rearrange("p b d -> p (b d)")[:, 0:CAP * PAIRS // 2])]
        low_hots = [low_hot[:, s, :, :, :] for s in range(2)] + [
            region.bitcast(bf16).rearrange("p (k m n) -> p k m n", k=CAP, m=4)
            for region in (desk[:, DESK + 3 * ROWS - CAP * 2 * P:DESK + 3 * ROWS],
                           dev.rearrange("p b d -> p (b d)")[:, 0:CAP * 2 * P])]
        assert CAP * PAIRS // 2 + CAP * 2 * P <= 2 * ROWS
        A += CAP * 4 * P
        count_strip = arena[:, A:A + NPAD // 2].bitcast(bf16).rearrange("p (b n) -> p b n", n=P)
        A += NPAD // 2
        source_strip = arena[:, A:A + NPAD].rearrange("p (b n) -> p b n", n=P)
        A += NPAD
        light_strip = arena[:, A:A + NPAD]
        KEYS = CAP * PAIRS + CAP * 4 * P + NPAD // 2
        key_hots = arena[:, KEYS:KEYS + SLOTS * GROUP * P].rearrange("p (s e) -> p s e", s=SLOTS)
        assert 3 * COLS + 2 * SPAN <= BUILD - COLS // 2
        loc_t = arena[:, BUILD - COLS // 2:BUILD].bitcast(f16).rearrange("p (j q) -> p j q", q=P)
        loc_rows = dev.rearrange("p b d -> p (b d)")[:, 0:SLOTS * GROUP * P // 2].bitcast(f16).rearrange("p (s e) -> p s e", s=SLOTS)
        source_strips = [source_strip, desk[:, SLOTS * GROUP * P:SLOTS * GROUP * P + NPAD].rearrange("p (b n) -> p b n", n=P), source_strip]
        assert SLOTS * GROUP * P + NPAD <= DESK
        count_ring = arena[:, 0:RING * NPAD // 2].bitcast(bf16).rearrange("p (s b n) -> p s b n", s=RING, n=P)
        light_ring = [arena[:, s * NPAD:(s + 1) * NPAD] for s in range(3)] + [desk[:, s * NPAD:(s + 1) * NPAD] for s in range(2)]
        stage = sb("stage", [P, RING, D])
        rel_pair = sb("rel_pair", [P, 2, CAP])
        idx_slot = sb("idx_slot", [P, SLOTS, GROUP], i32)
        key_slot = desk[:, DESK - P:DESK - P + SLOTS * GROUP].bitcast(i32).rearrange("p (s j) -> p s j", s=SLOTS)
        found = sb("found", [1, 4])
        worst = sb("worst", [1, 1])
        row_i = agg[0:1, :, :].rearrange("a b d -> a (b d)")[:, 0:COLS].bitcast(i32)

        acc = ctx.enter_context(nc.psum_tensor("acc", [P, ACC_BANKS * BANK], f32))
        work = ctx.enter_context(nc.psum_tensor("work", [P, 4, BANK], f32))
        acc_blocks = acc[:, 0:BLOCKS * D].rearrange("p (b d) -> p b d", d=D)
        light_bank = [acc[:, k * BANK:(k + 1) * BANK] for k in range(ACC_BANKS)] + [work[:, k, :] for k in range(TCHUNKS - ACC_BANKS)]
        dense_bank = [work[:, k, :] for k in range(4)] + [acc[:, 0:BANK]]

        edges_in, weights_in, x_in = sem("edges_in"), sem("weights_in"), sem("x_in")
        pool_const, row_const = sem("pool_const"), sem("row_const")
        vec_step = sem("vec_step")
        fields_ready = sem("fields_ready")
        ends_ready = sem("ends_ready")
        edge_turned = sem("edge_turned")
        edge_copied = sem("edge_copied")
        below_ready, below_summed = sem("below_ready"), sem("below_summed")
        ends_stored, ends_loaded = sem("ends_stored"), sem("ends_loaded")
        loc_ready, loc_stored = sem("loc_ready"), sem("loc_stored")
        loc_in = [sem(f"loc_in{s}") for s in range(SLOTS)]
        key_hot = [sem(f"key_hot{s}") for s in range(SLOTS)]
        key_sum = [sem(f"key_sum{s}") for s in range(SLOTS)]
        group_ready = sem("group_ready")
        framed = sem("framed")
        frames_copied = sem("frames_copied")
        setup_done = sem("setup_done")
        var_ready, std_ready = sem("var_ready"), sem("std_ready")
        node_ready = sem("node_ready")
        turned = sem("turned")
        turned_copied = sem("turned_copied")
        product = sem("product")
        product_copied = sem("product_copied")
        proj_taken = sem("proj_taken")
        table_ready, table_stored = sem("table_ready"), sem("table_stored")
        node_tab_ready, node_tab_stored = sem("node_tab_ready"), sem("node_tab_stored")
        rel_stored = [sem(f"rel_stored{k}") for k in range(4)]
        acc_free = sem("acc_free")
        acc_ready = sem("acc_ready")
        slot_open = [sem(f"slot_open{s}") for s in range(SLOTS)]
        idx_ready = [sem(f"idx_ready{s}") for s in range(SLOTS)]
        gathered = [sem(f"gathered{s}") for s in range(SLOTS)]
        hot_ready = [sem(f"hot_ready{s}") for s in range(SLOTS)]
        gate_in = [sem(f"gate_in{s}") for s in range(SLOTS)]
        gate_out = [sem(f"gate_out{s}") for s in range(SLOTS)]
        rel_ready = sem("rel_ready")
        low_ready = sem("low_ready")
        build_hot = [sem(f"build_hot{s}") for s in range(2)]
        weighted0, weighted = sem("weighted0"), sem("weighted")
        stripe_sum, stripe_taken = sem("stripe_sum"), sem("stripe_taken")
        count_full, count_stored = sem("count_full"), sem("count_stored")
        source_full = sem("source_full")
        light_turned, light_taken = sem("light_turned"), sem("light_taken")
        light_full, light_stored = sem("light_full"), sem("light_stored")
        inverted = sem("inverted")
        planes_ready = sem("planes_ready")
        count_in = [sem(f"count_in{s}") for s in range(RING)]
        dense_sum, dense_taken = sem("dense_sum"), sem("dense_taken")
        light_in = [sem(f"light_in{s}") for s in range(RING)]
        light_used = [sem(f"light_used{s}") for s in range(RING)]
        staged = sem("staged")
        light_sum, light_copied = sem("light_sum"), sem("light_copied")
        all_idx, all_hot, all_open = sem("all_idx"), sem("all_hot"), sem("all_open")
        all_rows = [sem(f"all_rows{p}") for p in range(PASSES)]
        all_gate_in, all_gate_out = sem("all_gate_in"), sem("all_gate_out")
        slot_taken, store_turn = sem("slot_taken"), sem("store_turn")
        out_stored = sem("out_stored")

        TURNS = ITERS + 1
        EDGE_FIELDS = 4
        FIELD_BANKS = -(-CHUNKS // PER_BANK)
        EDGE_BANKS = EDGE_FIELDS * FIELD_BANKS
        FULL_CHUNKS = E // (P * P)
        MORE = (E - FULL_CHUNKS * P * P) // P
        REST = E - FULL_CHUNKS * P * P - MORE * P
        GATE_BANKS = -(-BLOCKS // 2)
        SAGE1_BANKS = TCHUNKS
        SAGE2_BANKS = -(-BLOCKS // 4)
        REL_BANKS = 2 * BLOCKS
        KEY_BANK = 2
        NEAR = {0: 0, 3: 1}
        HOTS = (2, 4)
        def turns_of(u, slots, building):
            turns = []
            for j in range(u // BLOCK_SLOTS):
                if (j + 2) * BLOCK_SLOTS <= slots and j == u // BLOCK_SLOTS - 1:
                    c = 2 * (u % BLOCK_SLOTS)
                    turns.append((j, range(c, min(c + 2, TCHUNKS)), False))
            j = block_ended(u, slots, building)
            if j is not None and (j + 2) * BLOCK_SLOTS > slots:
                turns.append((j, range(TCHUNKS), True))
            return turns

        assert 2 * BLOCK_SLOTS >= TCHUNKS and ROUND_BLOCKS == 3
        COUNTS, WEIGHTS = 0, 1

        def schedule(eng, stretch):
            with eng.Fori(0, EDGE_ROUNDS) as r:
                stretch(r, ROUND, ROUND)
            stretch(EDGE_ROUNDS, LAST, BLOCK_SLOTS)

        def stripes_of(u, building):
            return range(PER_SLOT * u, PER_SLOT * (u + 1)) if u < building else ()

        def block_ended(u, slots, building):
            if u and u % BLOCK_SLOTS == 0 and u <= building:
                return u // BLOCK_SLOTS - 1
            return u // BLOCK_SLOTS if u == slots - 1 == building - 1 else None

        block = ctx.enter_context(nc.Block())

        @block.sync
        def _(sp):
            sp.wait_ge(pool_const, 4)
            for raw, field in ((dst_raw, dst), (src_raw, src), (et_raw, etype), (w_raw, weight)):
                a, b = FULL_CHUNKS * P * P, FULL_CHUNKS * P * P + MORE * P
                sp.dma_start(raw[:, 0:FULL_CHUNKS, :],
                             field[0:a].rearrange("(j q p) -> q j p", q=P, p=P)).then_inc(edges_in, 16)
                sp.dma_start(raw[0:MORE, FULL_CHUNKS, :],
                             field[a:b].rearrange("(q p) -> q p", p=P)).then_inc(edges_in, 16)
                sp.dma_start(raw[MORE:MORE + 1, FULL_CHUNKS, 0:REST],
                             field[b:E].rearrange("(a n) -> a n", a=1)).then_inc(edges_in, 16)
            sp.wait_ge(edge_copied, EDGE_BANKS + 1)
            sp.dma_start(ends_d.rearrange("k j q -> j k q"), ends_t).then_inc(ends_stored, 16)
            sp.wait_ge(ends_stored, 16)
            sp.dma_start(ends_row.rearrange("a k t -> a (k t)"), ends_d.rearrange("(a k) j q -> a (k j q)", a=1)).then_inc(ends_loaded, 16)

            def by_block(tab):
                return tab.rearrange("(b p) d -> p b d", p=P)

            sp.wait_ge(edge_copied, EDGE_BANKS + 3 + FIELD_BANKS)
            sp.dma_start(loc_d.rearrange("(j q) p -> q j p", q=P), loc_t).then_inc(loc_stored, 16)
            sp.wait_ge(table_ready, 1)
            sp.dma_start(by_block(key_tab), proj[:, :, 0:D]).then_inc(table_stored, 16)
            sp.dma_start(by_block(qv_tab), proj[:, :, D:3 * D]).then_inc(table_stored, 16)
            sp.wait_ge(setup_done, 1)
            far = sp.value_load(spread[0:1, 0:1], min_val=0, max_val=1)
            with sp.If(far == 0):
                def load_loc(s, g):
                    sp.dma_start(loc_rows[:, s, :], loc_d[bass.ds(g * GROUP, GROUP), :].rearrange("(a t) p -> a (t p)", a=1).to_broadcast([P, GROUP * P])).then_inc(loc_in[s], 16)

                def stretch(r, slots, building):
                    for u in range(slots):
                        s, i = u % SLOTS, r * ROUND_ITERS + u // SLOTS
                        sp.wait_ge(key_hot[s], i + 1)
                        sp.sem_inc(store_turn, 1)
                        load_loc(s, i * SLOTS + (SLOTS + s))
                        j = block_ended(u, slots, building)
                        if j is not None:
                            b = r * ROUND_BLOCKS + j
                            sp.wait_ge(count_full, b + 1)
                            sp.sem_inc(store_turn, 1)
                            sp.dma_start(count_d[bass.ds(b, 1), :, :].rearrange("a p n -> (a p) n"),
                                         count_strip.rearrange("p b n -> p (b n)")).then_inc(count_stored, 16)

                sp.sem_inc(count_stored, 16)
                sp.wait_ge(loc_stored, 16)
                for s in range(SLOTS):
                    load_loc(s, s)
                schedule(sp, stretch)
                sp.wait_ge(count_stored, 16 * BLOCKS + 16)
                sp.wait_ge(acc_ready, 1)
                for d in range(2):
                    with sp.Fori(0, ROUNDS) as r:
                        for s in range(RING):
                            sp.wait_ge(dense_sum, r * RING + (d * BLOCKS + s + 1))
                            sp.sem_inc(store_turn, 1)
                            sp.dma_start(count_ring[:, s, :, :].rearrange("p b n -> p (b n)"),
                                         count_d[bass.ds(r * RING + s, 1), :, :].rearrange("a p n -> (a p) n")).then_inc(count_in[s], 16)
            with sp.Else():
                sp.wait_ge(node_tab_ready, 1)
                sp.dma_start(by_block(node_tab[1]), H[:, :, :]).then_inc(node_tab_stored, 16)
                sp.wait_ge(node_tab_ready, 2)
                sp.dma_start(by_block(node_tab[2]), own[:, :, 0:D]).then_inc(node_tab_stored, 16)
            before = GATE_BANKS + SAGE1_BANKS + SAGE2_BANKS
            for b in range(BLOCKS):
                sp.wait_ge(product_copied, before + 2 * b + 2)
                sp.dma_start(rel_tab[b * P * R:(b + 1) * P * R, :].rearrange("(p r) d -> p (r d)", r=R),
                             rel_out[:, b % 4, :]).then_inc(rel_stored[b % 4], 16)
            with sp.If(far == 0):
                sp.sem_inc(light_stored, 16)
                with sp.Fori(0, BLOCKS) as b:
                    sp.wait_ge(light_full, b + 1)
                    sp.sem_inc(store_turn, 1)
                    sp.dma_start(light_d[bass.ds(b, 1), :, :].rearrange("a p n -> (a p) n"), light_strip).then_inc(light_stored, 16)
                sp.wait_ge(light_stored, 16 * BLOCKS + 16)
                for d in range(3):
                    with sp.Fori(0, ROUNDS) as r:
                        for s in range(RING):
                            if d == 0 and s == 3:
                                sp.wait_ge(acc_ready, 4)
                            sp.wait_ge(light_used[s], r + (d * ROUNDS + 1))
                            sp.sem_inc(store_turn, 1)
                            sp.dma_start(light_ring[s], light_d[bass.ds(r * RING + s, 1), :, :].rearrange("a p n -> (a p) n")).then_inc(light_in[s], 16)
            with sp.Else():
                for k, (p, ready) in enumerate(((4, H), (5, agg), (6, agg))):
                    sp.wait_ge(node_tab_ready, 3 + k)
                    sp.dma_start(by_block(node_tab[p]), ready[:, :, :]).then_inc(node_tab_stored, 16)
            sp.wait_ge(table_ready, 2)
            sp.dma_start(out[0:FULL_BLOCKS * P, :].rearrange("(b p) d -> p b d", p=P),
                         X[:, 0:FULL_BLOCKS, :]).then_inc(out_stored, 16)
            sp.dma_start(out[FULL_BLOCKS * P:N, :], X[0:TAIL, FULL_BLOCKS, :]).then_inc(out_stored, 16)
            sp.wait_ge(out_stored, 32)

        @block.gpsimd
        def _(pool):
            pool.memset(dst_raw, int(FAR)).then_inc(pool_const, 1)
            pool.memset(src_raw, 0).then_inc(pool_const, 1)
            pool.memset(et_raw, 0).then_inc(pool_const, 1)
            pool.memset(w_raw, 0.0).then_inc(pool_const, 1)
            pool.memset(X[:, FULL_BLOCKS, :], 0.0).then_inc(pool_const, 1)
            pool.memset(shifts[:, :], 0.0).then_inc(pool_const, 1)
            pool.memset(ones[:, :], 1.0).then_inc(pool_const, 1)
            pool.memset(zeros[:, :], 0.0).then_inc(pool_const, 1)
            pool.wait_ge(pool_const, 8)
            pool.affine_select(out=ident[:, :], in_=ident[:, :], compare_op=ALU.not_equal, fill=1.0,
                               base=0, pattern=[[-1, P]], channel_multiplier=1).then_inc(pool_const, 1)
            for to, step in ((stripe0[:, :], STRIPE), (pair0[:, :], PAIRS), (iota_w[:, :], 1), (iota_h[:, :], 1), (iota_f, 1)):
                pool.iota(to, pattern=[[step, to.shape[1]]], base=0, channel_multiplier=0,
                          allow_small_or_imprecise_dtypes=True).then_inc(pool_const, 1)
            pool.iota(part[:, :], pattern=[[0, 1]], base=0, channel_multiplier=1,
                      allow_small_or_imprecise_dtypes=True).then_inc(pool_const, 1)
            pool.wait_ge(setup_done, 1)
            far = pool.value_load(spread[0:1, 0:1], min_val=0, max_val=1)

            def gather(to, tab, idx, done):
                pool.indirect_dma_start(to, None, tab, bass.IndirectOffsetOnAxis(ap=idx, axis=0)).then_inc(done, 16)

            def near(p):
                q = NEAR[p]
                with pool.Fori(0, ITERS) as i:
                    for s in range(SLOTS):
                        pool.wait_ge(idx_ready[s], i + (q * TURNS + 1))
                        pool.wait_ge(slot_open[s], i + (q * TURNS + 1))
                        pool.sem_inc(slot_taken, 1)
                        for j in range(GROUP):
                            if p == 0:
                                gather(qv_rows[:, s, j, :], qv_tab, idx_slot[:, s, j:j + 1], gathered[s])
                            else:
                                gather(rows[:, s, j, :], rel_tab, idx_slot[:, s, j:j + 1], gathered[s])

            def everywhere(p):
                tab = (qv_tab, node_tab[1], node_tab[2], rel_tab, node_tab[4], node_tab[5], node_tab[6])[p]
                if p not in (0, 3):
                    pool.wait_ge(node_tab_stored, 16 * (1, 2, 3, 4, 5)[p - 1 if p < 3 else p - 2])
                with pool.Fori(0, TILES) as t:
                    pool.wait_ge(all_idx, t + (p * TILES + 1))
                    pool.sem_inc(slot_taken, 1)
                    gather((qv_rows if p == 0 else rows)[:, 0, 0, :], tab, idx_slot[:, 0, 0:1], all_rows[p])
                    if p == 0:
                        gather(key_rows[:, 0, 0, :], key_tab, key_slot[:, 0, 0:1], all_rows[p])

            pool.wait_ge(table_stored, 32)
            with pool.If(far == 0):
                near(0)
            with pool.Else():
                for p in range(3):
                    everywhere(p)
            for k in range(4):
                pool.wait_ge(rel_stored[k], 16 * len(range(k, BLOCKS, 4)))
            with pool.If(far == 0):
                near(3)
            with pool.Else():
                for p in range(3, PASSES):
                    everywhere(p)

        @block.vector
        def _(vec):
            n = 0

            def done(last):
                nonlocal n
                last.then_inc(vec_step, 1)
                n += 1
                vec.wait_ge(vec_step, n)

            vec.memset(hT[D:D + 1, :], 1.0).then_inc(row_const, 1)
            vec.memset(planes[:, :, 3 * D:], 1.0)
            vec.memset(b2_sb[:, :], 0.0).then_inc(row_const, 1)
            vec.wait_ge(edges_in, 12 * 16)
            vec.tensor_copy(src_f, src_raw)
            vec.tensor_copy(rel_f, et_raw)
            done(vec.tensor_copy(dst_f, dst_raw))
            vec.scalar_tensor_tensor(rel_f, src_f, float(R), rel_f, ALU.mult, ALU.add).then_inc(fields_ready, 1)
            vec.tensor_reduce(tile_min[:, :], dst_f, AX.X, ALU.min)
            done(vec.scalar_tensor_tensor(real_f, dst_f, float(NPAD), dst_f, ALU.is_lt, ALU.mult))
            done(vec.tensor_reduce(row_max[:, :], real_f, AX.X, ALU.max))
            vec.tensor_tensor(tile_max[:, :], row_max[:, :], tile_min[:, :], ALU.max).then_inc(ends_ready, 1)
            vec.wait_ge(ends_ready, 1)
            vec.wait_ge(pool_const, 15)
            for k, end in enumerate((tile_max, tile_min)):
                vec.tensor_tensor(below[k], end[:, :].unsqueeze(1).to_broadcast([P, BELOW, CHUNKS]),
                                  stripe0[:, :].unsqueeze(2).to_broadcast([P, BELOW, CHUNKS]), ALU.is_lt).then_inc(vec_step, 1)
                n += 1
            vec.wait_ge(vec_step, n)
            for k in range(2):
                vec.tensor_reduce(n_below[:, k, :], below[k], AX.X, ALU.add).then_inc(below_ready, 1)
            m = 0
            for field in (dst_col, to_col, rel_col[:, :], w_col):
                for c in range(FIELD_BANKS):
                    vec.wait_ge(edge_turned, m + 1)
                    size = min(PER_BANK, CHUNKS - PER_BANK * c) * P
                    vec.tensor_copy(field[:, c * BANK:c * BANK + size], work[:, m % 3, 0:size]).then_inc(edge_copied, 1)
                    m += 1
            vec.wait_ge(edge_turned, m + 1)
            vec.tensor_copy(ends_t, work[0:CHUNKS, m % 3, 0:2 * P].rearrange("p (k q) -> p k q", k=2)).then_inc(edge_copied, 1)
            m += 1
            vec.wait_ge(edge_copied, m)
            vec.tensor_copy(src_col[:, :], to_col)
            done(vec.tensor_scalar(key_col[:, :], dst_col, float(N - 1), None, ALU.min))
            done(vec.tensor_scalar(high_i, src_col[:, :], 7, None, ALU.arith_shift_right))
            done(vec.tensor_copy(high_f, high_i))
            vec.scalar_tensor_tensor(low_col[:, :], high_f, -float(P), to_col, ALU.mult, ALU.add)
            vec.scalar_tensor_tensor(pair_col[:, :], dst_col, float(BLOCKS), high_f, ALU.mult, ALU.add)
            left = w_col
            for k in range(3):
                done(vec.tensor_copy(w_half[k], left))
                done(vec.tensor_copy(w_plane[k][:, :], w_half[k]))
                if k < 2:
                    rest = (left_f, left2_f)[k]
                    done(vec.tensor_tensor(rest, left, w_plane[k][:, :], ALU.subtract))
                    left = rest
            vec.wait_ge(ends_loaded, 16)
            vec.tensor_copy(group_row.rearrange("a (g j) -> a g j", j=TEAM),
                            ends_row[:, 0, :].rearrange("a (g j) -> a g j", j=TEAM)[:, :, 0:1].to_broadcast([1, COLS // TEAM, TEAM])).then_inc(group_ready, 1)
            for c in range(2):
                vec.wait_ge(edge_turned, m + 1)
                vec.tensor_scalar(first_i[:, c * COLS // 2:(c + 1) * COLS // 2], work[:, m % 3, 0:COLS // 2],
                                  float(N - 1), float(STEP_MUL), ALU.min, ALU.mult).then_inc(edge_copied, 1)
                m += 1
            vec.wait_ge(edge_copied, m)
            done(vec.tensor_scalar(high_i, first_i, STEP_SHIFT, None, ALU.arith_shift_right))
            done(vec.tensor_copy(first_f, high_i))
            vec.scalar_tensor_tensor(dst_loc[:, :], first_f, -float(STEP), dst_col, ALU.mult, ALU.add).then_inc(loc_ready, 1)
            done(vec.tensor_scalar(row_i[:, :], group_row, float(N - 1), float(STEP_MUL), ALU.min, ALU.mult))
            done(vec.tensor_scalar(frame_row[:, :], row_i[:, :], STEP_SHIFT, None, ALU.arith_shift_right))
            for c in range(FIELD_BANKS):
                size = min(PER_BANK, CHUNKS - PER_BANK * c)
                vec.wait_ge(edge_turned, m + 1)
                vec.tensor_copy(loc_t[:, PER_BANK * c:PER_BANK * c + size, :],
                                work[:, m % 3, 0:size * P].rearrange("p (j q) -> p j q", q=P)).then_inc(edge_copied, 1)
                m += 1
            vec.tensor_tensor(check_row[:, 0:COLS - 1], ends_row[:, 1, 0:COLS - 1], ends_row[:, 0, 1:COLS], ALU.subtract)
            done(vec.tensor_scalar(check2_row, ends_row[:, 0, :], float(NPAD), None, ALU.is_lt))
            done(vec.tensor_reduce(found[:, 0:1], check_row[:, 0:COLS - 1], AX.X, ALU.max))
            done(vec.tensor_tensor(check_row, ends_row[:, 1, :], group_row, ALU.subtract))
            done(vec.tensor_tensor(check_row, check_row, check2_row, ALU.mult))
            done(vec.tensor_scalar(check_row, check_row, -float(P - STEP), None, ALU.add))
            done(vec.tensor_reduce(found[:, 1:2], check_row, AX.X, ALU.max))
            done(vec.tensor_tensor(check_row, ends_row[:, 1, :], ends_row[:, 0, :], ALU.subtract))
            done(vec.tensor_scalar(check_row, check_row, 1.0, None, ALU.is_lt))
            done(vec.tensor_tensor(check_row, check_row, check2_row, ALU.mult))
            done(vec.tensor_reduce(found[:, 2:3], check_row, AX.X, ALU.max))
            vec.wait_ge(below_summed, 1)
            sums = work[0:1, 3, 0:2 * BELOW].rearrange("a (k g) -> a k g", k=2)
            done(vec.tensor_copy(n_below[0:1, :, :], sums))
            vec.tensor_copy(first_tile[:, :], n_below[0:1, 0, 0:ALL_STRIPES])
            done(vec.tensor_tensor(check_row[:, 0:ALL_STRIPES], n_below[0:1, 1, 1:BELOW], n_below[0:1, 0, 0:ALL_STRIPES], ALU.subtract))
            done(vec.tensor_scalar(check_row[:, 0:ALL_STRIPES], check_row[:, 0:ALL_STRIPES], -float(CAP), None, ALU.add))
            done(vec.tensor_reduce(found[:, 3:4], check_row[:, 0:ALL_STRIPES], AX.X, ALU.max))
            done(vec.tensor_reduce(worst[:, :], found[:, :], AX.X, ALU.max))
            vec.tensor_scalar(spread[:, :], worst[:, :], 0.0, None, ALU.is_gt).then_inc(setup_done, 1)
            vec.wait_ge(setup_done, 1)
            far = vec.value_load(spread[0:1, 0:1], min_val=0, max_val=1)

            wide = [P, BLOCKS, D]

            def layernorm(nth):
                done(vec.tensor_reduce(row_sum[:, :], X[:, :, :], AX.X, ALU.add))
                done(vec.tensor_scalar(mean[:, :], row_sum[:, :], 1.0 / D, None, ALU.mult))
                done(vec.tensor_tensor(dev[:, :, :], X[:, :, :], mean[:, :].unsqueeze(2).to_broadcast(wide), ALU.subtract))
                done(vec.tensor_tensor(sq[:, :, :], dev[:, :, :], dev[:, :, :], ALU.mult))
                done(vec.tensor_reduce(sq_sum[:, :], sq[:, :, :], AX.X, ALU.add))
                vec.tensor_scalar(var[:, :], sq_sum[:, :], 1.0 / D, EPS, ALU.mult, ALU.add).then_inc(var_ready, 1)
                vec.wait_ge(std_ready, nth)
                done(vec.reciprocal(rstd[:, :], std[:, :]))
                done(vec.tensor_tensor(dev[:, :, :], dev[:, :, :], rstd[:, :].unsqueeze(2).to_broadcast(wide), ALU.mult))

            def split(of):
                done(vec.tensor_copy(plane[0], of))
                done(vec.tensor_tensor(dev[:, :, :], of, plane[0], ALU.subtract))
                done(vec.tensor_copy(plane[1], dev[:, :, :]))
                done(vec.tensor_tensor(sq[:, :, :], dev[:, :, :], plane[1], ALU.subtract))
                vec.tensor_copy(plane[2], sq[:, :, :]).then_inc(planes_ready, 1)

            def build_stripe(kind, r, x):
                first = r * (ROUND_BLOCKS * STRIPES)
                g = r * (ROUND_BLOCKS * STRIPES) + x
                step = kind * ALL_STRIPES + x + 1
                low, pair = low_hots[x % HOTS[kind]], pair_hots[x % HOTS[kind]]
                t = vec.value_load(first_tile[0:1, bass.ds(g, 1)], min_val=0, max_val=COLS - CAP)
                vec.wait_ge(stripe_sum, first + (step + 2 - HOTS[kind]))
                vec.tensor_scalar(rel_pair[:, x % 2, :], pair_col[:, bass.ds(t, CAP)], pair0[:, bass.ds(g, 1)], None,
                                  ALU.subtract).then_inc(rel_ready, 1)
                for c in range(CAP):
                    last = vec.tensor_scalar(low[:, c, 0, :], iota_h[:, 0:P], low_col[:, bass.ds(t + c, 1)], None, ALU.is_equal)
                last.then_inc(low_ready, 1)
                vec.wait_ge(rel_ready, first + step)
                for c in range(CAP):
                    last = vec.tensor_scalar(pair[:, c, :], iota_h[:, :], rel_pair[:, x % 2, c:c + 1], None, ALU.is_equal)
                last.then_inc(build_hot[x % 2], 1)
                if kind == WEIGHTS:
                    vec.wait_ge(low_ready, first + step)
                    vec.tensor_tensor(low[:, :, 1, :], low[:, :, 0, :],
                                      w_plane[0][:, bass.ds(t, CAP)].unsqueeze(2).to_broadcast([P, CAP, P]), ALU.mult).then_inc(weighted0, 1)

            def take_frames(nth):
                vec.wait_ge(framed, nth)
                vec.tensor_copy(keys[:, :, :], acc[:, :].rearrange("p (b d) -> p b d", d=D)).then_inc(frames_copied, 1)

            def near(p):
                q = kind = NEAR[p]
                idx = rel_col if p == 3 else src_col
                ROWS16 = 16 * GROUP
                before = q * ITERS * ROWS16

                def indices(s, t):
                    vec.tensor_copy(idx_slot[:, s, :], idx[:, bass.ds(t, GROUP)]).then_inc(idx_ready[s], 1)

                def turned_hots(s, i):
                    vec.wait_ge(loc_in[s], i * 16 + 16)
                    vec.wait_ge(key_sum[s], i + 1)
                    vec.tensor_scalar(key_hots[:, s, :], loc_rows[:, s, :], part[:, :], None, ALU.is_equal).then_inc(key_hot[s], 1)

                def stretch(r, slots, building):
                    for u in range(slots):
                        s, i = u % SLOTS, r * ROUND_ITERS + u // SLOTS
                        share = stripes_of(u, building)
                        if p == 0:
                            turned_hots((s + 1) % SLOTS, i + (s + 1) // SLOTS)
                        early = 1 if p == 0 else PER_SLOT
                        for x in share[:early]:
                            build_stripe(kind, r, x)
                        vec.wait_ge(slot_open[s], i + (q * TURNS + 1))
                        for j in range(GROUP):
                            t = i * (SLOTS * GROUP) + (s * GROUP + j)
                            last = vec.tensor_scalar(hot[:, s, j, :], iota_w[:, :], dst_loc[:, bass.ds(t, 1)], None, ALU.is_equal)
                        if p:
                            last.then_inc(hot_ready[s], 1)
                        vec.wait_ge(gathered[s], i * ROWS16 + (before + ROWS16))
                        indices(s, i * (SLOTS * GROUP) + (SLOTS * GROUP + s * GROUP))
                        if p == 0:
                            vec.wait_ge(key_sum[s], i + 2)
                            vec.tensor_tensor(key_rows[:, s, :, :], work[:, KEY_BANK, :].rearrange("p (j d) -> p j d", d=D),
                                              qv_rows[:, s, :, 0:D], ALU.add).then_inc(gate_in[s], 1)
                        for x in share[early:]:
                            build_stripe(kind, r, x)
                        if p == 0:
                            vec.wait_ge(gate_out[s], i + 1)
                            vec.tensor_tensor(rows[:, s, :, :], key_rows[:, s, :, :],
                                              qv_rows[:, s, :, D:2 * D], ALU.mult).then_inc(hot_ready[s], 1)

                for s in range(SLOTS):
                    indices(s, s * GROUP)
                if p == 0:
                    take_frames(1)
                    turned_hots(0, 0)
                schedule(vec, stretch)
                if p == 0:
                    for s in range(SLOTS):
                        vec.wait_ge(loc_in[s], 16 * (ITERS + 1))
                take_frames(q + 2)

            def everywhere(p):
                idx = rel_col if p == 3 else key_col if p >= 4 else src_col
                to = to_col if p >= 4 else dst_col
                with vec.Fori(0, TILES) as t:
                    vec.wait_ge(all_open, t + (p * (TILES + 1) + 1))
                    if p == 0:
                        vec.tensor_copy(key_slot[:, 0, 0:1], key_col[:, bass.ds(t, 1)])
                    vec.tensor_copy(idx_slot[:, 0, 0:1], idx[:, bass.ds(t, 1)]).then_inc(all_idx, 1)
                    last = vec.tensor_scalar(wide_hot, iota_f, to[:, bass.ds(t, 1)],
                                             w_col[:, bass.ds(t, 1)] if p >= 4 else 1.0, ALU.is_equal, ALU.mult)
                    if p:
                        last.then_inc(all_hot, 1)
                    if p == 0:
                        vec.wait_ge(all_rows[p], t * 32 + 32)
                        vec.tensor_tensor(key_rows[:, 0, 0, :], key_rows[:, 0, 0, :],
                                          qv_rows[:, 0, 0, 0:D], ALU.add).then_inc(all_gate_in, 1)
                        vec.wait_ge(all_gate_out, t + 1)
                        vec.tensor_tensor(rows[:, 0, 0, :], key_rows[:, 0, 0, :],
                                          qv_rows[:, 0, 0, D:2 * D], ALU.mult).then_inc(all_hot, 1)

            def invert():
                vec.tensor_scalar(degree[:, :], degree[:, :], 1.0, None, ALU.max).then_inc(inverted, 1)
                vec.wait_ge(inverted, 1)
                vec.reciprocal(rdeg[:, :], degree[:, :]).then_inc(inverted, 1)
                vec.wait_ge(inverted, 2)

            def means(d):
                with vec.If(far == 0):
                    with vec.Fori(0, ROUNDS) as r:
                        for s in range(RING):
                            vec.wait_ge(dense_sum, r * RING + (d * BLOCKS + s + 1 + RING))
                            if d == 0:
                                vec.tensor_copy(degree[:, bass.ds(r * RING + s, 1)], dense_bank[s][:, 3 * D:3 * D + 1])
                            vec.tensor_reduce(agg[:, bass.ds(r * RING + s, 1), :].rearrange("p a f -> p (a f)"),
                                              dense_bank[s][:, 0:3 * D].rearrange("p (k f) -> p f k", k=3),
                                              AX.X, ALU.add).then_inc(dense_taken, 1)
                    vec.wait_ge(dense_taken, (d + 1) * BLOCKS + RING)
                    if d == 0:
                        invert()
                    vec.tensor_tensor(agg[:, :, :], agg[:, :, :], rdeg[:, :].unsqueeze(2).to_broadcast(wide), ALU.mult).then_inc(acc_free, 1)
                with vec.Else():
                    everywhere(1 + d)
                    vec.wait_ge(acc_ready, 2 + d)
                    if d == 0:
                        invert()
                    vec.tensor_tensor(agg[:, :, :], acc_blocks, rdeg[:, :].unsqueeze(2).to_broadcast(wide), ALU.mult).then_inc(acc_free, 1)

            vec.wait_ge(x_in, 32)
            layernorm(1)
            vec.tensor_scalar(H[:, :, :], dev[:, :, :], 0.0, None, ALU.max).then_inc(node_ready, 1)
            vec.wait_ge(product_copied, GATE_BANKS)
            done(vec.tensor_tensor(X[:, :, :], X[:, :, :], proj[:, :, 3 * D:4 * D], ALU.add))
            vec.wait_ge(table_stored, 32)
            with vec.If(far == 0):
                near(0)
            with vec.Else():
                everywhere(0)
            vec.sem_inc(dense_taken, RING)
            vec.wait_ge(acc_ready, 1)
            vec.tensor_copy(degree[:, :], acc[:, CNT0:CNT0 + BLOCKS])
            vec.tensor_tensor(X[:, :, :], X[:, :, :], acc_blocks, ALU.add).then_inc(acc_free, 1)
            vec.wait_ge(acc_free, 1)

            layernorm(2)
            vec.wait_ge(turned, TCHUNKS)
            vec.tensor_scalar(H[:, :, :], dev[:, :, :], 0.0, None, ALU.max).then_inc(node_ready, 1)
            vec.wait_ge(node_ready, 2)
            vec.sem_inc(node_tab_ready, 1)
            split(H[:, :, :])
            means(0)
            vec.wait_ge(product_copied, GATE_BANKS + SAGE1_BANKS + SAGE2_BANKS)
            vec.sem_inc(node_tab_ready, 1)
            split(own[:, :, 0:D])
            vec.wait_ge(turned, 3 * TCHUNKS)
            means(1)
            vec.wait_ge(acc_free, 3)
            done(vec.tensor_tensor(agg[:, :, :], agg[:, :, :], own[:, :, D:2 * D], ALU.add))
            vec.sem_inc(proj_taken, 1)
            done(vec.scalar_tensor_tensor(X[:, :, :], agg[:, :, :], 0.0, X[:, :, :], ALU.max, ALU.add))

            layernorm(3)
            vec.tensor_scalar(H[:, :, :], dev[:, :, :], 0.0, None, ALU.max).then_inc(node_ready, 1)
            for k in range(4):
                vec.wait_ge(rel_stored[k], 16 * len(range(k, BLOCKS, 4)))
            with vec.If(far == 0):
                near(3)
            with vec.Else():
                everywhere(3)
            vec.wait_ge(acc_ready, 4)
            done(vec.tensor_tensor(X[:, :, :], X[:, :, :], acc_blocks, ALU.add))

            layernorm(4)
            vec.wait_ge(turned, 4 * TCHUNKS)
            done(vec.tensor_scalar(H[:, :, :], dev[:, :, :], 0.0, None, ALU.max))
            vec.sem_inc(node_tab_ready, 1)
            vec.tensor_copy(light[:, :, :], H[:, :, :]).then_inc(acc_free, 1)
            vec.wait_ge(acc_free, 4)
            for d in range(3):
                with vec.If(far == 0):
                    vec.wait_ge(light_sum, d + 1)
                    for c in range(ACC_BANKS):
                        vec.tensor_copy(hT[0:D, c * BANK:(c + 1) * BANK], light_bank[c][0:D, :]).then_inc(light_copied, 1)
                    vec.wait_ge(acc_ready, 5 + d)
                with vec.Else():
                    everywhere(4 + d)
                    vec.wait_ge(acc_ready, 5 + d)
                if d < 2:
                    done(vec.tensor_copy(agg[:, :, :], acc_blocks))
                    vec.sem_inc(node_tab_ready, 1)
                    vec.tensor_tensor(light[:, :, :], light[:, :, :], acc_blocks, ALU.add).then_inc(acc_free, 1)
                    vec.wait_ge(acc_free, 5 + d)
                else:
                    done(vec.tensor_tensor(light[:, :, :], light[:, :, :], acc_blocks, ALU.add))
            vec.scalar_tensor_tensor(X[:, :, :], light[:, :, :], 0.25, X[:, :, :], ALU.mult, ALU.add).then_inc(table_ready, 1)

        @block.scalar
        def _(act):
            act.wait_ge(pool_const, 5)
            act.dma_start(X[:, 0:FULL_BLOCKS, :],
                          x[0:FULL_BLOCKS * P, :].rearrange("(b p) d -> p b d", p=P)).then_inc(x_in, 16)
            act.dma_start(X[0:TAIL, FULL_BLOCKS, :], x[FULL_BLOCKS * P:N, :]).then_inc(x_in, 16)
            for k, (w, b) in enumerate(((w_key, b_key), (w_query, b_query), (w_value, b_value), (w_skip, b_skip))):
                act.dma_start(w_gate[0:D, k * D:(k + 1) * D], w).then_inc(weights_in, 16)
                act.dma_start(w_gate[D:D + 1, k * D:(k + 1) * D], b.rearrange("(a n) -> a n", a=1)).then_inc(weights_in, 16)
            act.dma_start(w1l_sb[:, :], w1_l).then_inc(weights_in, 16)
            act.dma_start(w1r_sb[:, :], w1_r).then_inc(weights_in, 16)
            act.dma_start(b1_sb[:, :], b1.rearrange("(n a) -> n a", a=1)).then_inc(weights_in, 16)
            act.dma_start(w2_sb[:, 0:D], w2_l).then_inc(weights_in, 16)
            act.dma_start(w2_sb[:, D:2 * D], w2_r).then_inc(weights_in, 16)
            act.wait_ge(row_const, 2)
            act.dma_start(b2_sb[:, D:2 * D], b2.rearrange("(a n) -> a n", a=1)).then_inc(weights_in, 16)
            act.dma_start(rel_sb[:, :, :], w_rel.rearrange("r i o -> i r o")).then_inc(weights_in, 16)
            act.wait_ge(setup_done, 1)
            far = act.value_load(spread[0:1, 0:1], min_val=0, max_val=1)

            def root(nth):
                act.wait_ge(var_ready, nth)
                act.activation(std[:, :], var[:, :], ACT.Sqrt).then_inc(std_ready, 1)

            def take_turned(nth, to):
                for c in range(TCHUNKS):
                    size = min(PER_BANK, BLOCKS - PER_BANK * c) * P
                    act.wait_ge(turned, nth * TCHUNKS + c + 1)
                    act.activation(to[0:D, c * BANK:c * BANK + size], work[0:D, c % 4, 0:size], ACT.Copy).then_inc(turned_copied, 1)

            def take_stripe(kind, r, x):
                b, k = r * ROUND_BLOCKS + x // STRIPES, x % STRIPES
                first = r * (ROUND_BLOCKS * STRIPES)
                if kind == COUNTS and k == 0:
                    act.wait_ge(count_stored, b * 16 + 16)
                act.wait_ge(stripe_sum, first + (kind * ALL_STRIPES + x + 3))
                strip = count_strip if kind == COUNTS else source_strips[x // STRIPES]
                act.activation(strip[:, :, k * STRIPE:(k + 1) * STRIPE], work[:, x % 2, 0:PAIRS].rearrange("p (n b) -> p b n", n=STRIPE),
                               ACT.Copy).then_inc(stripe_taken, 1)
                if k == STRIPES - 1:
                    act.wait_ge(stripe_taken, first + (kind * ALL_STRIPES + x + 3))
                    act.sem_inc((count_full, source_full)[kind], 1)

            def weight_stripe(r, x):
                g = r * (ROUND_BLOCKS * STRIPES) + x
                t = act.value_load(first_tile[0:1, bass.ds(g, 1)], min_val=0, max_val=COLS - CAP)
                act.wait_ge(low_ready, r * (ROUND_BLOCKS * STRIPES) + (ALL_STRIPES + x + 1))
                low = low_hots[x % HOTS[WEIGHTS]]
                for c in range(CAP):
                    for m in range(1, 3):
                        last = act.activation(low[:, c, 1 + m, :], low[:, c, 0, :], ACT.Copy,
                                              scale=w_plane[m][:, bass.ds(t + c, 1)])
                last.then_inc(weighted, 1)

            def take_block(b, chunks):
                if chunks[0] == 0:
                    act.wait_ge(light_stored, b * 16 + 16)
                for c in chunks:
                    size = min(PER_BANK, BLOCKS - PER_BANK * c) * P
                    act.wait_ge(light_turned, b * TCHUNKS + (c + 1))
                    act.activation(light_strip[:, c * BANK:c * BANK + size], work[:, 2 + c % 2, 0:size], ACT.Copy).then_inc(light_taken, 1)
                if chunks[-1] == TCHUNKS - 1:
                    act.wait_ge(light_taken, b * TCHUNKS + (TCHUNKS + 1))
                    act.sem_inc(light_full, 1)

            def near(p):
                kind = NEAR[p]
                LAG = (1, 2)[kind]

                def stretch(r, slots, building):
                    taken, later = 0, []
                    for u in range(slots):
                        s, i = u % SLOTS, r * ROUND_ITERS + u // SLOTS
                        if p == 0:
                            act.wait_ge(gate_in[s], i + 1)
                            act.activation(key_rows[:, s, :, :], key_rows[:, s, :, :], ACT.Sigmoid).then_inc(gate_out[s], 1)
                        for x in stripes_of(u, building):
                            if kind == WEIGHTS:
                                weight_stripe(r, x)
                            if x >= LAG:
                                take_stripe(kind, r, x - LAG)
                                taken = x - LAG + 1
                            for j, chunks in later:
                                take_block(r * ROUND_BLOCKS + j, chunks)
                            later = []
                        j = block_ended(u, slots, building)
                        if j is not None:
                            for x in range(taken, (j + 1) * STRIPES):
                                take_stripe(kind, r, x)
                                taken = x + 1
                        if kind == WEIGHTS:
                            for j, chunks, awaited in turns_of(u, slots, building):
                                if awaited or u == slots - 1:
                                    take_block(r * ROUND_BLOCKS + j, chunks)
                                else:
                                    later.append((j, chunks))

                schedule(act, stretch)

            root(1)
            take_turned(0, hT)
            for c in range(GATE_BANKS):
                k = min(2, BLOCKS - 2 * c)
                act.wait_ge(product, c + 1)
                act.activation(proj[:, 2 * c:2 * c + k, :], work[:, c % 4, 0:k * 4 * D].rearrange("p (b n) -> p b n", b=k),
                               ACT.Copy).then_inc(product_copied, 1)
            act.wait_ge(product_copied, GATE_BANKS)
            act.sem_inc(table_ready, 1)

            with act.If(far == 0):
                act.sem_inc(stripe_taken, 2)
                act.sem_inc(light_taken, 1)
                near(0)
            with act.Else():
                with act.Fori(0, TILES) as t:
                    act.wait_ge(all_gate_in, t + 1)
                    act.activation(key_rows[:, 0, 0, :], key_rows[:, 0, 0, :], ACT.Sigmoid).then_inc(all_gate_out, 1)
            root(2)
            take_turned(1, hT)
            take_turned(2, mT)
            before = GATE_BANKS
            for c in range(SAGE1_BANKS):
                size = min(BANK, NPAD - BANK * c)
                act.wait_ge(product, before + c + 1)
                act.activation(gT[:, c * BANK:c * BANK + size], work[:, c % 4, 0:size], ACT.Relu,
                               bias=b1_sb[:, 0:1]).then_inc(product_copied, 1)
            before += SAGE1_BANKS
            for c in range(SAGE2_BANKS):
                k = min(4, BLOCKS - 4 * c)
                act.wait_ge(product, before + c + 1)
                act.activation(own[:, 4 * c:4 * c + k, :], work[:, c % 4, 0:k * 2 * D].rearrange("p (b n) -> p b n", b=k),
                               ACT.Copy).then_inc(product_copied, 1)
            before += SAGE2_BANKS
            root(3)
            take_turned(3, hT)
            act.wait_ge(proj_taken, 1)
            for c in range(REL_BANKS):
                b = c // 2
                if b >= 4:
                    act.wait_ge(rel_stored[b % 4], 16 * (b // 4))
                act.wait_ge(product, before + c + 1)
                act.activation(rel_out[:, b % 4, (c % 2) * BANK:(c % 2 + 1) * BANK], work[:, c % 4, :], ACT.Copy).then_inc(product_copied, 1)
            with act.If(far == 0):
                near(3)
            root(4)
            with act.If(far == 0):
                for d in range(3):
                    act.wait_ge(acc_free, 4 + d)
                    cur = H if d == 0 else agg
                    with act.Fori(0, ROUNDS) as r:
                        for s in range(RING):
                            act.wait_ge(light_used[s], r + (d * ROUNDS + 1))
                            act.activation(stage[:, s, :], cur[:, bass.ds(r * RING + s, 1), :].rearrange("p a f -> p (a f)"), ACT.Copy).then_inc(staged, 1)
                    act.wait_ge(light_sum, d + 1)
                    for c in range(ACC_BANKS, TCHUNKS):
                        size = min(BANK, NPAD - BANK * c)
                        act.activation(hT[0:D, c * BANK:c * BANK + size], light_bank[c][0:D, 0:size], ACT.Copy).then_inc(light_copied, 1)

        @block.tensor
        def _(pe):
            pe.wait_ge(pool_const, 15)
            pe.wait_ge(row_const, 2)
            pe.wait_ge(fields_ready, 1)
            m = 0
            for field in (dst_f, src_f, rel_f, w_raw):
                for c in range(FIELD_BANKS):
                    if m >= 3:
                        pe.wait_ge(edge_copied, m - 2)
                    for j in range(min(PER_BANK, CHUNKS - PER_BANK * c)):
                        last = pe.transpose(work[:, m % 3, j * P:(j + 1) * P], field[:, PER_BANK * c + j, :], ident[:, :])
                    last.then_inc(edge_turned, 1)
                    m += 1
                if m == 2 * FIELD_BANKS:
                    pe.wait_ge(below_ready, 2)
                    pe.matmul(work[0:1, 3, 0:2 * BELOW], ones[:, 0:1], n_below.rearrange("p k g -> p (k g)"), start=True, stop=True).then_inc(below_summed, 1)
            pe.wait_ge(edge_copied, m - 2)
            pe.wait_ge(ends_ready, 1)
            pe.transpose(work[0:CHUNKS, m % 3, 0:P], tile_min[:, :], ident[:, :])
            pe.transpose(work[0:CHUNKS, m % 3, P:2 * P], tile_max[:, :], ident[:, :]).then_inc(edge_turned, 1)
            m += 1
            pe.wait_ge(group_ready, 1)
            for c in range(2):
                pe.wait_ge(edge_copied, m - 2)
                pe.matmul(work[:, m % 3, 0:COLS // 2], ones[0:1, :], group_row[:, c * COLS // 2:(c + 1) * COLS // 2], start=True, stop=True).then_inc(edge_turned, 1)
                m += 1
            pe.wait_ge(loc_ready, 1)
            for c in range(FIELD_BANKS):
                pe.wait_ge(edge_copied, m - 2)
                for j in range(min(PER_BANK, CHUNKS - PER_BANK * c)):
                    at = (PER_BANK * c + j) * P
                    last = pe.transpose(work[:, m % 3, j * P:(j + 1) * P], dst_loc[:, at:at + P], ident[:, :])
                last.then_inc(edge_turned, 1)
                m += 1
            pe.wait_ge(edge_copied, m)
            pe.wait_ge(setup_done, 1)
            far = pe.value_load(spread[0:1, 0:1], min_val=0, max_val=1)

            def turn(nth, of):
                for c in range(TCHUNKS):
                    if c >= 4:
                        pe.wait_ge(turned_copied, nth * TCHUNKS + c - 3)
                    for j in range(min(PER_BANK, BLOCKS - PER_BANK * c)):
                        last = pe.transpose(work[0:D, c % 4, j * P:(j + 1) * P], of[:, PER_BANK * c + j, :], ident[:, :])
                    last.then_inc(turned, 1)

            def add(lhs, rhs, at):
                return pe.matmul(acc[:, at], lhs, rhs, start=False, stop=True, skip_group_check=True)

            def zero():
                for k in range(ACC_BANKS):
                    last = pe.matmul(acc[:, k * BANK:(k + 1) * BANK], zeros[:, 0:P], zeros[:, :], start=True, stop=True, skip_group_check=True)
                return last

            def framed_now():
                add(zeros[:, 0:P], zeros[:, 0:1], slice(ACC_BANKS * BANK - 1, ACC_BANKS * BANK)).then_inc(framed, 1)

            def finish():
                add(zeros[:, 0:P], zeros[:, 0:1], slice(ACC_BANKS * BANK - 1, ACC_BANKS * BANK)).then_inc(acc_ready, 1)

            def build_stripe(kind, r, k):
                first = r * (ROUND_BLOCKS * STRIPES)
                pe.wait_ge(build_hot[k % 2], r * (ROUND_BLOCKS * STRIPES // 2) + (kind * ALL_STRIPES // 2 + k // 2 + 1))
                pe.wait_ge(stripe_taken, first + (kind * ALL_STRIPES + k + 1))
                planes_of = (0,)
                if kind == WEIGHTS:
                    pe.wait_ge(weighted0, first + (k + 1))
                    pe.wait_ge(weighted, first + (k + 1))
                    planes_of = (1, 2, 3)
                for c in range(CAP):
                    for m in planes_of:
                        last = pe.matmul(work[:, k % 2, 0:PAIRS], low_hots[k % HOTS[kind]][:, c, m, :], pair_hots[k % HOTS[kind]][:, c, :],
                                         start=c == 0 and m == planes_of[0], stop=c == CAP - 1 and m == planes_of[-1])
                last.then_inc(stripe_sum, 1)

            def turn_block(b, strip, chunks):
                if chunks[0] == 0:
                    pe.wait_ge(source_full, b + 1)
                for c in chunks:
                    if c != 1:
                        pe.wait_ge(light_taken, b * TCHUNKS + max(c, 1))
                    for j in range(min(PER_BANK, BLOCKS - PER_BANK * c)):
                        last = pe.transpose(work[:, 2 + c % 2, j * P:(j + 1) * P], strip[:, PER_BANK * c + j, :], ident[:, :])
                    last.then_inc(light_turned, 1)

            def near(p):
                q = NEAR[p]
                if p == 0:
                    zero()
                    for a in range(FRAMES):
                        size = min(P, NPAD - a * STEP)
                        pe.matmul(acc[0:size, a * D:(a + 1) * D], hT[:, a * STEP:a * STEP + size], w_gate[:, 0:D],
                                  start=False, stop=True, skip_group_check=True)
                    framed_now()
                    pe.wait_ge(frames_copied, 1)
                zero().then_inc(slot_open[0], 1)
                for s in range(1, SLOTS):
                    pe.sem_inc(slot_open[s], 1)

                def frames_of(s, i):
                    return [pe.value_load(frame_row[0:1, bass.ds(i * (SLOTS * GROUP) + (s * GROUP + j * TEAM), 1)], min_val=0, max_val=FRAMES - 1)
                            for j in range(FRAMED)]

                def take_keys(s, i, before=None, at=None):
                    frames = frames_of(s, i)
                    if before is not None:
                        pe.wait_ge(gate_in[before], at)
                    pe.wait_ge(key_hot[s], i + 1)
                    for j in range(GROUP):
                        last = pe.matmul(work[:, KEY_BANK, j * D:(j + 1) * D], key_hots[:, s, j * P:(j + 1) * P],
                                         keys[:, bass.ds(frames[j // TEAM], 1), :].rearrange("p a d -> p (a d)"), start=True, stop=True)
                    last.then_inc(key_sum[s], 1)

                def stretch(r, slots, building):
                    for u in range(slots):
                        s, i = u % SLOTS, r * ROUND_ITERS + u // SLOTS
                        for x in stripes_of(u, building):
                            build_stripe(q, r, x)
                        if p == 0:
                            take_keys((s + 1) % SLOTS, i + (s + 1) // SLOTS, s, i + 1)
                        if q == WEIGHTS:
                            for j, chunks, _ in turns_of(u, slots, building):
                                turn_block(r * ROUND_BLOCKS + j, source_strips[j], chunks)
                        frames = frames_of(s, i)
                        pe.wait_ge(hot_ready[s], i + (q * ITERS + 1))
                        if p:
                            pe.wait_ge(gathered[s], i * (16 * GROUP) + (ITERS + 1) * 16 * GROUP)
                        for j in range(GROUP):
                            last = add(hot[:, s, j, :], rows[:, s, j, :], bass.ds(frames[j // TEAM] * D, D))
                        last.then_inc(slot_open[s], 1)

                if p == 0:
                    pe.sem_inc(stripe_sum, 2)
                    for s in range(SLOTS):
                        pe.sem_inc(key_sum[s], 1)
                    take_keys(0, 0)
                    pe.sem_inc(dense_sum, RING)
                else:
                    for s in range(RING):
                        pe.sem_inc(light_used[s], 1)
                schedule(pe, stretch)
                if p == 0:
                    pe.wait_ge(stripe_taken, ALL_STRIPES + 2)
                else:
                    pe.wait_ge(light_taken, BLOCKS * TCHUNKS + 1)
                framed_now()
                pe.wait_ge(frames_copied, q + 2)
                for b in range(BLOCKS):
                    parts = [a for a in range(FRAMES) if abs(a * STEP - b * P) < P]
                    for a in parts:
                        at = P - (a * STEP - b * P)
                        pe.matmul(acc[:, b * D:(b + 1) * D], shifts[:, at:at + P], keys[:, a, :], start=a == parts[0], stop=a == parts[-1])
                finish()

            def everywhere(p):
                zero().then_inc(all_open, 1)
                with pe.Fori(0, TILES) as t:
                    pe.wait_ge(all_hot, t + (p * TILES + 1))
                    if p:
                        pe.wait_ge(all_rows[p], t * 16 + 16)
                    for b in range(ALL_BLOCKS):
                        lhs = wide_hot[:, b * P:(b + 1) * P]
                        last = add(lhs, rows[:, 0, 0, :], slice(b * D, (b + 1) * D))
                        if p == 0:
                            last = add(lhs, ones[:, 0:1], slice(CNT0 + b, CNT0 + b + 1))
                    last.then_inc(all_open, 1)
                finish()

            def counts(d):
                pe.wait_ge(planes_ready, d + 1)
                COLUMNS = 3 * D + (1 if d == 0 else 0)
                with pe.Fori(0, ROUNDS) as r:
                    for s in range(RING):
                        pe.wait_ge(count_in[s], r * 16 + (d * ROUNDS * 16 + 16))
                        pe.wait_ge(dense_taken, r * RING + (d * BLOCKS + s + 1))
                        for h in range(BLOCKS):
                            last = pe.matmul(dense_bank[s][:, 0:COLUMNS], count_ring[:, s, h, :], planes[:, h, 0:COLUMNS], start=h == 0, stop=h == BLOCKS - 1)
                        last.then_inc(dense_sum, 1)
                finish()

            def lights(d):
                for bank in light_bank:
                    pe.matmul(bank, zeros[:, 0:P], zeros[:, :], start=True, stop=True, skip_group_check=True)
                with pe.Fori(0, ROUNDS) as r:
                    for s in range(RING):
                        pe.wait_ge(light_in[s], r * 16 + (d * ROUNDS * 16 + 16))
                        pe.wait_ge(staged, r * RING + (d * BLOCKS + s + 1))
                        for c in range(TCHUNKS):
                            size = min(BANK, NPAD - BANK * c)
                            last = pe.matmul(light_bank[c][0:D, 0:size], stage[:, s, :], light_ring[s][:, c * BANK:c * BANK + size],
                                             start=False, stop=True, skip_group_check=True)
                        last.then_inc(light_used[s], 1)
                pe.matmul(light_bank[-1][0:D, BANK - 1:BANK], zeros[:, 0:D], zeros[:, 0:1], start=False, stop=True,
                          skip_group_check=True).then_inc(light_sum, 1)
                pe.wait_ge(light_copied, (d + 1) * TCHUNKS)
                for b in range(BLOCKS):
                    pe.transpose(acc[:, b * D:(b + 1) * D], hT[0:D, b * P:(b + 1) * P], ident[0:D, 0:D])
                finish()

            pe.wait_ge(weights_in, 15 * 16)
            pe.wait_ge(node_ready, 1)
            turn(0, H)
            pe.wait_ge(turned_copied, TCHUNKS)
            for c in range(GATE_BANKS):
                if c >= 4:
                    pe.wait_ge(product_copied, c - 3)
                for k in range(min(2, BLOCKS - 2 * c)):
                    b = 2 * c + k
                    last = pe.matmul(work[:, c % 4, k * 4 * D:(k + 1) * 4 * D], hT[:, b * P:(b + 1) * P], w_gate[:, :], start=True, stop=True)
                last.then_inc(product, 1)
            pe.wait_ge(product_copied, GATE_BANKS)
            with pe.If(far == 0):
                near(0)
            with pe.Else():
                everywhere(0)

            pe.wait_ge(node_ready, 2)
            turn(1, H)
            pe.wait_ge(turned_copied, 2 * TCHUNKS)
            pe.wait_ge(acc_free, 1)
            with pe.If(far == 0):
                counts(0)
            with pe.Else():
                everywhere(1)
            pe.wait_ge(acc_free, 2)
            turn(2, agg)
            pe.wait_ge(turned_copied, 3 * TCHUNKS)
            before = GATE_BANKS
            for c in range(SAGE1_BANKS):
                if c >= 4:
                    pe.wait_ge(product_copied, before + c - 3)
                size = min(BANK, NPAD - BANK * c)
                pe.matmul(work[:, c % 4, 0:size], w1l_sb[:, :], mT[:, c * BANK:c * BANK + size], start=True, stop=False)
                pe.matmul(work[:, c % 4, 0:size], w1r_sb[:, :], hT[0:D, c * BANK:c * BANK + size], start=False, stop=True).then_inc(product, 1)
            before += SAGE1_BANKS
            pe.wait_ge(product_copied, before)
            for c in range(SAGE2_BANKS):
                if c >= 4:
                    pe.wait_ge(product_copied, before + c - 3)
                for k in range(min(4, BLOCKS - 4 * c)):
                    b = 4 * c + k
                    at = work[:, c % 4, k * 2 * D:(k + 1) * 2 * D]
                    pe.matmul(at, gT[:, b * P:(b + 1) * P], w2_sb[:, :], start=True, stop=False)
                    last = pe.matmul(at, ones[0:1, :], b2_sb[:, :], start=False, stop=True)
                last.then_inc(product, 1)
            before += SAGE2_BANKS
            pe.wait_ge(product_copied, before)
            with pe.If(far == 0):
                counts(1)
            with pe.Else():
                everywhere(2)

            pe.wait_ge(acc_free, 3)
            pe.wait_ge(node_ready, 3)
            turn(3, H)
            pe.wait_ge(turned_copied, 4 * TCHUNKS)
            for c in range(REL_BANKS):
                if c >= 4:
                    pe.wait_ge(product_copied, before + c - 3)
                pe.matmul(work[:, c % 4, :], hT[0:D, (c // 2) * P:(c // 2 + 1) * P],
                          rel_sb[:, (c % 2) * (R // 2):(c % 2 + 1) * (R // 2), :].rearrange("i r o -> i (r o)"),
                          start=True, stop=True).then_inc(product, 1)
            before += REL_BANKS
            pe.wait_ge(product_copied, before)
            with pe.If(far == 0):
                near(3)
            with pe.Else():
                everywhere(3)

            for d in range(3):
                pe.wait_ge(acc_free, 4 + d)
                with pe.If(far == 0):
                    lights(d)
                with pe.Else():
                    everywhere(4 + d)


_INS = ['x', 'src', 'dst', 'edge_type_16', 'edge_weight', 'L0_gnn_W_key', 'L0_gnn_b_key', 'L0_gnn_W_query', 'L0_gnn_b_query',
        'L0_gnn_W_value', 'L0_gnn_b_value', 'L0_gnn_W_skip', 'L0_gnn_b_skip', 'L1_gnn_W1_l', 'L1_gnn_b1', 'L1_gnn_W1_r',
        'L1_gnn_W2_l', 'L1_gnn_b2', 'L1_gnn_W2_r', 'L2_gnn_weight']


def kernel(**inputs):
    import numpy as _np
    import concourse.bacc as _bacc
    from concourse import mybir as _mybir
    from concourse.bass_utils import run_bass_kernel_spmd as _run

    nc = _bacc.Bacc("TRN2", target_bir_lowering=False, num_devices=1)
    arrays, args = {}, []
    for name in _INS:
        a = _np.ascontiguousarray(inputs[name])
        arrays[f"in_{name}_dram"] = a
        args.append(nc.dram_tensor(f"in_{name}_dram", a.shape, _mybir.dt.from_np(a.dtype), kind="ExternalInput").ap())
    args.append(nc.dram_tensor("out_0_dram", (N, D), _mybir.dt.float32, kind="ExternalOutput").ap())
    build(nc, *args)
    r = _run(nc, [arrays], core_ids=[0])
    return r.results[0]["out_0_dram"]
```
